# Optimizing a Trainium2 kernel written in Bass

```python
import numpy as np
import jax
import jax.numpy as jnp

def _softmax(x, axis=-1):
    return jax.nn.softmax(x, axis=axis)

def _gelu(x):
    return jax.nn.gelu(x, approximate=True)

def _silu(x):
    return jax.nn.silu(x)

def _sigmoid(x):
    return jax.nn.sigmoid(x)

def _layernorm(x, axis=-1, eps=1e-05):
    m = jnp.mean(x, axis=axis, keepdims=True)
    v = jnp.var(x, axis=axis, keepdims=True)
    return (x - m) / jnp.sqrt(v + eps)

def _scatter_add(tgt, idx, src, axis=0):
    return tgt.at[idx].add(src)

def _segment_sum(src, seg, n):
    return jax.ops.segment_sum(src, seg, n)
kernel_name = 'mk_adaln_d1_jaxref_r8_5af3c6'

def setup_inputs(seed: int=0):
    np.random.seed(seed)
    _w = jnp.asarray

    def _L0_attn_setup():
        import jax, jax.numpy as jnp
        import numpy as np
        B, T, D_MODEL, N_HEADS = (2, 256, 128, 16)
        key = jax.random.key(seed)
        ks = jax.random.split(key, 5)
        w_scale = 0.02
        return {'x': jax.random.normal(ks[0], (B, T, D_MODEL), jnp.float32), 'Wq': jax.random.normal(ks[1], (D_MODEL, D_MODEL), jnp.float32) * w_scale, 'Wk': jax.random.normal(ks[2], (D_MODEL, D_MODEL), jnp.float32) * w_scale, 'Wv': jax.random.normal(ks[3], (D_MODEL, D_MODEL), jnp.float32) * w_scale, 'Wo': jax.random.normal(ks[4], (D_MODEL, D_MODEL), jnp.float32) * w_scale}
    _L0_attn_in = _L0_attn_setup()

    def _L0_ffn_setup():
        import jax, jax.numpy as jnp
        import numpy as np
        B, S, H, E = (2, 1024, 128, 8)
        SCALE = 0.5
        key = jax.random.key(seed)
        k1, k2 = jax.random.split(key)
        x = jax.random.normal(k1, (B, S, H), dtype=jnp.float32)
        gate_w = jax.random.normal(k2, (E, H), dtype=jnp.float32) * 0.02
        coeff = SCALE * (1.0 + 0.05 * jnp.arange(E, dtype=jnp.float32))
        expert_w = coeff[:, None, None] * jnp.eye(H, dtype=jnp.float32)
        return {'x': x, 'gate_w': gate_w, 'expert_w': expert_w}
    _L0_ffn_in = _L0_ffn_setup()
    _L0_c = _w((lambda *s: np.random.randn(*s).astype(np.float32) * 0.05)(4, 128))
    _L0_wmod = _w((lambda *s: np.random.randn(*s).astype(np.float32) * 0.05)(128, 6 * 128) * 128 ** (-0.5))
    _d = {'L0_attn_x': _L0_attn_in['x'], 'L0_attn_Wq': _L0_attn_in['Wq'], 'L0_attn_Wk': _L0_attn_in['Wk'], 'L0_attn_Wv': _L0_attn_in['Wv'], 'L0_attn_Wo': _L0_attn_in['Wo'], 'L0_ffn_gate_w': _L0_ffn_in['gate_w'], 'L0_ffn_expert_w': _L0_ffn_in['expert_w'], 'L0_c': _L0_c, 'L0_wmod': _L0_wmod}
    _x0 = _d['L0_attn_x']
    _d['L0_attn_x'] = jax.random.normal(jax.random.fold_in(jax.random.key(seed), 1), (4, 512, 128), dtype=_x0.dtype)
    del _x0
    return _d

def reference(L0_attn_x, L0_attn_Wq, L0_attn_Wk, L0_attn_Wv, L0_attn_Wo, L0_ffn_gate_w, L0_ffn_expert_w, L0_c, L0_wmod):

    def _L0_attn_ref(x, Wq, Wk, Wv, Wo):
        import jax, jax.numpy as jnp
        import numpy as np
        B, T, D_MODEL, N_HEADS = (2, 256, 128, 16)
        Bv, Tv, _ = x.shape
        H = N_HEADS
        D = D_MODEL // H
        q = (x @ Wq.T).reshape(Bv, Tv, H, D).transpose(0, 2, 1, 3)
        k = (x @ Wk.T).reshape(Bv, Tv, H, D).transpose(0, 2, 1, 3)
        v = (x @ Wv.T).reshape(Bv, Tv, H, D).transpose(0, 2, 1, 3)
        scale = jnp.sqrt(jnp.asarray(D, jnp.float32))
        scores = jnp.einsum('bhqd,bhkd->bhqk', q, k) / scale
        slopes = jnp.asarray([2.0 ** (-8.0 * h / H) for h in range(1, H + 1)], jnp.float32)
        pos = jnp.arange(Tv)
        dist = jnp.abs(pos[None, :] - pos[:, None]).astype(jnp.float32)
        bias = -dist[None, :, :] * slopes[:, None, None]
        causal_mask = jnp.triu(jnp.ones((Tv, Tv), dtype=bool), 1)
        bias = jnp.where(causal_mask[None, :, :], -jnp.inf, bias)
        scores = scores + bias[None]
        attn = jax.nn.softmax(scores, axis=-1)
        out = jnp.einsum('bhqk,bhkd->bhqd', attn, v)
        out = out.transpose(0, 2, 1, 3).reshape(Bv, Tv, D_MODEL)
        return out @ Wo.T

    def _L0_ffn_ref(x, gate_w, expert_w):
        import jax, jax.numpy as jnp
        import numpy as np
        B, S, H, E = (2, 1024, 128, 8)
        SCALE = 0.5
        scores = jnp.einsum('bsh,eh->bse', x, gate_w)
        chosen = jnp.argmax(scores, axis=-1)
        onehot = jax.nn.one_hot(chosen, gate_w.shape[0], dtype=x.dtype)
        expert_out = jnp.einsum('bsh,efh->bsef', x, expert_w)
        return x + jnp.einsum('bsef,bse->bsf', expert_out, onehot)
    x = L0_attn_x
    mod = (_silu(L0_c) @ L0_wmod).reshape(L0_c.shape[0], 6, 1, -1)
    sa, ca, ga, sb, cb, gb = (mod[:, 0], mod[:, 1], mod[:, 2], mod[:, 3], mod[:, 4], mod[:, 5])
    ga = (2 * (ga >= 0) - 1) * jnp.maximum(jnp.abs(ga), 0.25)
    gb = (2 * (gb >= 0) - 1) * jnp.maximum(jnp.abs(gb), 0.25)
    h = _layernorm(x, axis=-1) * (1 + ca) + sa
    x = x + ga * _L0_attn_ref(h, L0_attn_Wq, L0_attn_Wk, L0_attn_Wv, L0_attn_Wo)
    h = _layernorm(x, axis=-1) * (1 + cb) + sb
    x = x + gb * _L0_ffn_ref(h, L0_ffn_gate_w, L0_ffn_expert_w)
    return x

_drawn_inputs = setup_inputs


def setup_inputs(seed=0):
    import zlib

    import numpy as np

    out = dict(_drawn_inputs(seed))
    spreads = {}
    factors = {'L0_attn_Wq': 8.0,
     'L0_attn_Wk': 8.0,
     'L0_attn_Wv': 8.0,
     'L0_attn_Wo': 8.0,
     'L0_ffn_gate_w': 4.057}
    for name, (base, spread) in spreads.items():
        noise = np.random.default_rng([zlib.crc32(name.encode()), seed]).standard_normal(out[name].shape)
        drawn = base * np.exp(spread * noise) if base else spread * noise
        out[name] = jnp.asarray(drawn.astype(out[name].dtype))
    for name, factor in factors.items():
        out[name] = (out[name] * factor).astype(out[name].dtype)
    return out
```

```python
import concourse.bass as bass
from concourse import mybir
from contextlib import ExitStack


def adaln_block(nc, x, wqT, wkT, wvT, woT, gwT, ewT, cT, wmod, qrows, krows, ident, identb, causal,
                choose, order, out):
    f32, bf16, i32 = mybir.dt.float32, mybir.dt.bfloat16, mybir.dt.int32
    ALU, ACT, AX = mybir.AluOpType, mybir.ActivationFunctionType, mybir.AxisListType

    B, T, D = x.shape
    H = 16
    DH = D // H
    E = gwT.shape[1]
    TT = T // 128
    PAIRS = H // 2
    QUADS = H // 4
    NP = B * PAIRS
    EPS = 1e-5
    R_BIAS, R_PROD, R_MAX, R_MASK = 0, 6, 54, 56
    R_END = 63
    QPART = [0, 0, 0, 1, 1, 2]
    KPART = [0, 1, 2, 0, 1, 0]
    LAG = 3
    AB, BB = 3, 2
    PW = 1280
    BSTEP = [[(t, t, 128, 128 * t) for t in range(TT)],
             [(0, 1, 384, 0), (2, 3, 128, 384)],
             [(1, 2, 256, 0)]]
    ASTEP = [[(3, 512, 0)], [(2, 384, 0), (0, 128, 384)], [(1, 256, 0)]]
    WIDTH = [512, 512, 256]
    P_AT = [0, 512, 1024]

    SIDE = {(0, 2): [("gate_onehot", 2)],
            (1, 0): [("mask0", 2)], (1, 1): [("mask1", 2)], (1, 2): [("mask2", 2)],
            (2, 0): [("mask3", 2)], (2, 2): [("mask4", 2), ("norm1", -1)],
            (3, 0): [("mask5", 2)], (3, 1): [("mask6", 2)], (3, 2): [("mask7", 2), ("query", -1)],
            (4, 1): [("key", -1)], (4, 2): [("attn", 1)],
            (5, 0): [("outproj", 1)], (5, 1): [("expert_back", 2)], (5, 2): [("attn_back", 1)],
            (6, 2): [("norm2", 1)], (7, 0): [("value", -1)], (7, 1): [("gate", 1)]}
    LAST = 8 * (B + 1) + 5 + 1

    def tasks(g, k):
        found = []
        if g < 0:
            return [(name, 0) for name in ("norm1", "query", "key", "value")] if k == 0 else []
        if g % 2 == 0 and k == 0 and 0 <= g // 2 - 3 < NP // 2:
            found.append(("heads_back", g // 2 - 3))
        if g % 2 == 0 and k == 1 and 0 <= g // 2 - 1 < NP // 2:
            found.append(("maxima", g // 2 - 1))
        for name, ahead in SIDE.get((g % 8, k), []):
            b = g // 8 - ahead
            if 0 <= b < B and not (ahead == -1 and b == 0):
                found.append((name, b))
        return found

    PLACES = [(-1, 0)] + [(g, k) for g in range(LAST) for k in range(3)]
    BY_DVE = {"heads_back", "attn_back", "gate", "expert_back"} | {f"mask{e}" for e in range(E)}
    USES = [t for p in PLACES for t in tasks(*p)]
    USE = {t: n for n, t in enumerate(USES)}

    def emptied(n):
        dve = sum(name in BY_DVE for name, _ in USES[:n])
        return dve, n - dve

    def by_dve(name, n):
        return emptied(USE[name, n] + 1)[0]

    def by_act(name, n):
        return emptied(USE[name, n] + 1)[1]

    NORMS = [("norm1", 0)]
    for g in range(LAST):
        for k in range(3):
            if g % 8 == 0 and k == 1 and g // 8 + 1 < B:
                NORMS.append(("norm1", g // 8 + 1))
            NORMS += [("norm2", b) for name, b in tasks(g, k) if name == "attn_back"]

    ctx = ExitStack()
    with ctx:
        def sb(name, shape, dt=f32):
            return ctx.enter_context(nc.sbuf_tensor(name, shape, dt))

        def pb(name):
            return ctx.enter_context(nc.psum_tensor(name, [128, 512], f32))

        def sem(name):
            return ctx.enter_context(nc.semaphore(name))

        wq_sb, wk_sb, wv_sb, wo_sb = (sb(n, [D, D]) for n in ("wq_sb", "wk_sb", "wv_sb", "wo_sb"))
        gw_sb = sb("gw_sb", [D, E])
        ew_in = sb("ew_in", [D, E, D])
        ew_sb = sb("ew_sb", [D, E, D])
        wmod_sb = sb("wmod_sb", [D, 6 * D])
        ident_sb = sb("ident_sb", [128, 128])
        identb_sb = sb("identb_sb", [128, 128], bf16)
        causal_sb = sb("causal_sb", [128, 512])
        choose_sb = sb("choose_sb", [E, E, 128], bf16)
        order_sb = sb("order_sb", [128, E])
        c_sb, c_exp, c_silu = sb("c_sb", [D, B]), sb("c_exp", [D, B]), sb("c_silu", [D, B])
        mod_sb = sb("mod_sb", [D, 6, B])
        gates = sb("gates", [D, 2, B])
        gate_sign, gate_size = sb("gate_sign", [D, 2, B]), sb("gate_size", [D, 2, B])
        x_sb = sb("x_sb", [128, B, TT, D])
        stats = sb("stats", [128, TT, 6])
        meanvar = sb("meanvar", [128, TT, 2])
        var_eps = sb("var_eps", [128, TT])
        half_bits = sb("half_bits", [128, TT], i32)
        rstd = sb("rstd", [128, TT])
        newton = sb("newton", [128, TT])
        normed = sb("normed", [128, TT, D])
        hT = sb("hT", [D, T])
        proj = sb("proj", [128, 2, T])
        rest = sb("rest", [128, 2, T])
        parts = sb("parts", [128, 2, 3, T], bf16)
        q_stack = [sb(f"q_stack{i}", [128, PAIRS * T], bf16) for i in range(2)]
        k_stack = [sb(f"k_stack{i}", [128, PAIRS * T], bf16) for i in range(2)]
        v_aug = sb("v_aug", [128, 2, TT, H, 32])
        scored = sb("scored", [128, 4, 512], bf16)
        maxima = sb("maxima", [128, 2, TT, 4])
        neg_max = sb("neg_max", [128, 2, TT, 4, 2], bf16)
        maxT = sb("maxT", [8, 2, T], bf16)
        probs = sb("probs", [128, 2, 4, PW])
        headsT = sb("headsT", [128, T])
        inv_sum = sb("inv_sum", [128, TT, 4])
        attn = sb("attn", [128, TT, D])
        attnT = sb("attnT", [D, T])
        backT = sb("backT", [D, 2, T])
        x1 = sb("x1", [128, 2, TT, D])
        h2T = sb("h2T", [D, T])
        top = sb("top", [128, TT])
        is_top = sb("is_top", [128, TT, E])
        rank = sb("rank", [128, TT, E])
        onehot = sb("onehot", [128, TT, E], bf16)
        onehotT = sb("onehotT", [E, T], bf16)
        masked = sb("masked", [D, 2, T])
        result = sb("result", [128, TT, D])
        scratch = nc.dram_tensor("parts_scratch", [B, 2, 3, 128, T], bf16).ap()

        a_bank = [pb(f"a_bank{i}") for i in range(AB)]
        b_bank = [pb(f"b_bank{i}") for i in range(BB)]
        v_bank = pb("v_bank")
        e_bank = pb("e_bank")
        side = pb("side")

        loaded_x = sem("loaded_x")
        loaded_c = sem("loaded_c")
        loaded_w = sem("loaded_w")
        loaded_rows = sem("loaded_rows")
        v_cleared = sem("v_cleared")
        experts_ready = sem("experts_ready")
        silu_exp = sem("silu_exp")
        silu_done = sem("silu_done")
        mod_summed = sem("mod_summed")
        mod_copied = sem("mod_copied")
        mod_ready = sem("mod_ready")
        rsqrt_begun = sem("rsqrt_begun")
        norm_done = sem("norm_done")
        side_filled = sem("side_filled")
        side_by_dve = sem("side_by_dve")
        side_by_act = sem("side_by_act")
        parts_done = sem("parts_done")
        parts_stored = [sem(f"parts_stored{i}") for i in range(2)]
        stacked = [sem(f"stacked{i}") for i in range(2)]
        a_filled = sem("a_filled")
        a_emptied = sem("a_emptied")
        b_filled = sem("b_filled")
        b_emptied = sem("b_emptied")
        maxima_split = sem("maxima_split")
        max_rows = [sem(f"max_rows{i}") for i in range(2)]
        zeroed = sem("zeroed")
        v_filled = sem("v_filled")
        v_emptied = sem("v_emptied")
        onehot_ready = sem("onehot_ready")
        experts_fed = sem("experts_fed")
        e_emptied = sem("e_emptied")
        stored = sem("stored")
        dve_step = sem("dve_step")
        pool_step = sem("pool_step")

        LOADED_W = 16 * 13
        block = ctx.enter_context(nc.Block())

        @block.sync
        def _(sp):
            sp.dma_start(c_sb[:, :], cT).then_inc(loaded_c, 16)
            for t in range(TT):
                sp.dma_start(x_sb[:, 0, t, :], x[0, 128 * t:128 * t + 128, :]).then_inc(loaded_x, 16)
            for dst, src in ((wmod_sb[:, :], wmod), (ident_sb[:, :], ident), (wq_sb[:, :], wqT),
                             (wk_sb[:, :], wkT), (wv_sb[:, :], wvT), (causal_sb[:, :], causal),
                             (identb_sb[:, :], identb), (ew_in[:, :, :], ewT), (wo_sb[:, :], woT),
                             (gw_sb[:, :], gwT), (choose_sb[:, :, :], choose), (order_sb[:, :], order)):
                sp.dma_start(dst, src).then_inc(loaded_w, 16)
            for i in range(2):
                for par in range(2):
                    at = 64 * par
                    sp.dma_start(q_stack[i][at:at + R_PROD, :], qrows[par, 0:R_PROD, :]).then_inc(loaded_rows, 16)
                    sp.dma_start(k_stack[i][at:at + R_PROD, :], krows[par, 0:R_PROD, :]).then_inc(loaded_rows, 16)
                    sp.dma_start(k_stack[i][at + R_MAX:at + R_END, :], krows[par, R_PROD:, :]).then_inc(loaded_rows, 16)
                    sp.dma_start(q_stack[i][at + R_MASK:at + R_END, :], qrows[par, R_PROD:, :]).then_inc(loaded_rows, 16)
                if i == 0:
                    sp.dma_start(x_sb[:, 1:B, :, :], x[1:B].rearrange("b (t p) d -> p b t d", p=128)).then_inc(loaded_w, 16)

            def stack(b):
                for s, st in ((0, q_stack[b % 2]), (1, k_stack[b % 2])):
                    sp.wait_ge(parts_done, 2 * b + s + 1)
                    for n in range(3):
                        sp.dma_start(scratch[b, s, n], parts[:, s, n, :]).then_inc(parts_stored[s], 16)
                    if b >= 2 and s == 0:
                        sp.wait_ge(b_filled, 3 * PAIRS * 2 * (b - 1))
                    sp.wait_ge(parts_stored[s], 48 * (b + 1))
                    for n, part in enumerate(KPART if s else QPART):
                        for par in range(2):
                            at = 64 * par + R_PROD + DH * n
                            src = scratch[b, s, part, 64 * par:64 * par + 64, :]
                            sp.dma_start(st[at:at + DH, :], src.rearrange("(d j) t -> d (j t)", d=DH))\
                              .then_inc(stacked[b % 2], 16)

            for g, k in PLACES:
                for name, n in tasks(g, k):
                    if name == "maxima":
                        sp.wait_ge(side_by_act, by_act(name, n))
                        for c in range(4):
                            pair = (4 * n + c) // 2 % PAIRS
                            at = 64 * (c % 2) + R_MAX
                            dst = q_stack[n // QUADS % 2][at:at + 2, pair * T:(pair + 1) * T]
                            sp.dma_start(dst, maxT[2 * c:2 * c + 2, n % 2, :]).then_inc(max_rows[n % 2], 16)
                    if name == "key":
                        stack(n)
                    if name == "expert_back":
                        sp.wait_ge(side_by_dve, by_dve(name, n))
                        sp.dma_start(out[n].rearrange("(t p) d -> p t d", p=128), result[:, :, :]).then_inc(stored, 16)
            sp.wait_ge(stored, 16 * B)

        @block.gpsimd
        def _(pool):
            steps = [0]

            def link(ins):
                steps[0] += 1
                ins.then_inc(pool_step, 1)
                pool.wait_ge(pool_step, steps[0])

            def norm(n, src):
                pool.wait_ge(rsqrt_begun, n + 1)
                for _ in range(3):
                    link(nc.gpsimd.tensor_tensor(newton[:, :], rstd[:, :], rstd[:, :], ALU.mult))
                    link(nc.gpsimd.tensor_tensor(newton[:, :], newton[:, :], var_eps[:, :], ALU.mult))
                    link(nc.gpsimd.tensor_scalar(newton[:, :], newton[:, :], -0.5, 1.5, ALU.mult, ALU.add))
                    link(nc.gpsimd.tensor_tensor(rstd[:, :], rstd[:, :], newton[:, :], ALU.mult))
                if n >= 1:
                    pool.wait_ge(side_filled, USE[NORMS[n - 1]] + 1)
                for t in range(TT):
                    last = nc.gpsimd.tensor_scalar(normed[:, t, :], src[:, t, :], meanvar[:, t, 0:1],
                                                   rstd[:, t:t + 1], ALU.subtract, ALU.mult)
                last.then_inc(norm_done, 1)

            def split(s, b):
                pool.wait_ge(side_by_act, by_act("key" if s else "query", b))
                if b >= 1:
                    pool.wait_ge(parts_stored[s], 48 * b)
                part = parts[:, s, :, :]
                link(nc.gpsimd.tensor_scalar(part[:, 0, :], proj[:, s, :], 1.0, None, ALU.mult))
                link(nc.gpsimd.tensor_tensor(rest[:, s, :], proj[:, s, :], part[:, 0, :], ALU.subtract))
                link(nc.gpsimd.tensor_scalar(part[:, 1, :], rest[:, s, :], 1.0, None, ALU.mult))
                nc.gpsimd.tensor_tensor(part[:, 2, :], rest[:, s, :], part[:, 1, :], ALU.subtract)\
                    .then_inc(parts_done, 1)

            nc.gpsimd.memset(v_aug[:, :, :, :, :], 0.0).then_inc(v_cleared, 1)
            pool.wait_ge(v_cleared, 1)
            nc.gpsimd.memset(v_aug[:, :, :, :, DH:DH + 1], 1.0).then_inc(v_cleared, 1)
            norms = 0
            norm(norms, x_sb[:, 0, :, :])
            norms += 1
            split(0, 0)
            split(1, 0)
            pool.wait_ge(loaded_w, LOADED_W)
            nc.gpsimd.tensor_tensor(ew_sb[:, :, :], ew_in[:, :, :],
                                    ident_sb[:, :].unsqueeze(1).broadcast_to([128, E, 128]), ALU.add)\
                .then_inc(experts_ready, 1)
            for g in range(LAST):
                for k in range(3):
                    if k == 0 and 0 <= g - LAG < NP:
                        pair = g - LAG
                        for par in range(2):
                            pool.wait_ge(b_emptied, 6 * pair + par + 1)
                            diag = probs[:, pair // 2 % 2, 2 * (pair % 2) + par, 0:512]\
                                .rearrange("p (t q) -> p t q", t=TT)
                            nc.gpsimd.affine_select(out=diag, in_=diag, compare_op=ALU.is_ge, fill=0.0, base=0,
                                                    pattern=[[0, TT], [1, 128]], channel_multiplier=-1)\
                                .then_inc(zeroed, 1)
                    if g % 8 == 0 and k == 1 and g // 8 + 1 < B:
                        norm(norms, x_sb[:, g // 8 + 1, :, :])
                        norms += 1
                    for name, b in tasks(g, k):
                        if name == "query":
                            split(0, b)
                        if name == "key":
                            split(1, b)
                        if name == "attn_back":
                            norm(norms, x1[:, b % 2, :, :])
                            norms += 1

        @block.tensor
        def _(pe):
            def fill(task):
                dve, act = emptied(USE[task])
                if dve:
                    pe.wait_ge(side_by_dve, dve)
                if act:
                    pe.wait_ge(side_by_act, act)

            def turned(dst, src, idn, n=TT):
                for t in range(n):
                    last = nc.tensor.transpose(dst[:, 128 * t:128 * t + 128], src(t), idn)
                return last

            def feed_expert(e, b):
                pe.wait_ge(side_by_dve, by_dve(f"mask{e}", b))
                if e == 0:
                    pe.wait_ge(experts_ready, 1)
                    if b >= 1:
                        pe.wait_ge(e_emptied, b)
                nc.tensor.matmul(e_bank[:, :], ew_sb[:, e, :], masked[:, e % 2, :], start=(e == 0),
                                 stop=(e == E - 1)).then_inc(experts_fed, 1)

            def task(name, n):
                if name.startswith("mask"):
                    e = int(name[4:])
                    if e >= 1:
                        feed_expert(e - 1, n)
                fill((name, n))
                if name == "norm1" or name == "norm2":
                    pe.wait_ge(norm_done, NORMS.index((name, n)) + 1)
                    last = turned(side, lambda t: normed[:, t, :], ident_sb[:, :])
                if name in ("query", "key", "value"):
                    pe.wait_ge(side_by_act, by_act("norm1", n))
                if name == "query":
                    last = nc.tensor.matmul(side[:, :], wq_sb[:, :], hT[:, :], start=True, stop=True)
                if name == "key":
                    last = nc.tensor.matmul(side[:, :], wk_sb[:, :], hT[:, :], start=True, stop=True)
                if name == "value":
                    for t in range(TT):
                        last = nc.tensor.matmul(side[:, 128 * t:128 * t + 128], hT[:, 128 * t:128 * t + 128],
                                                wv_sb[:, :], start=True, stop=True)
                if name == "maxima":
                    pe.wait_ge(maxima_split, n + 1)
                    last = turned(side[0:8, 0:256].bitcast(bf16),
                                  lambda t: neg_max[:, n % 2, t, :, :].rearrange("p c s -> p (c s)"), identb_sb[:, :])
                if name == "heads_back":
                    pe.wait_ge(v_emptied, n + 1)
                    last = turned(side, lambda t: headsT[:, 128 * t:128 * t + 128], ident_sb[:, :])
                if name == "attn":
                    pe.wait_ge(side_by_dve, by_dve("heads_back", QUADS * n + QUADS - 1))
                    last = turned(side, lambda t: attn[:, t, :], ident_sb[:, :])
                if name == "outproj":
                    pe.wait_ge(side_by_act, by_act("attn", n))
                    last = nc.tensor.matmul(side[:, :], wo_sb[:, :], attnT[:, :], start=True, stop=True)
                if name == "attn_back":
                    pe.wait_ge(side_by_act, by_act("outproj", n))
                    last = turned(side, lambda t: backT[:, 0, 128 * t:128 * t + 128], ident_sb[:, :])
                if name == "gate":
                    pe.wait_ge(side_by_act, by_act("norm2", n))
                    for t in range(TT):
                        last = nc.tensor.matmul(side[:, E * t:E * t + E], h2T[:, 128 * t:128 * t + 128],
                                                gw_sb[:, :], start=True, stop=True)
                if name == "gate_onehot":
                    pe.wait_ge(onehot_ready, n + 1)
                    last = turned(side[0:E, 0:256].bitcast(bf16), lambda t: onehot[:, t, :], identb_sb[:, :])
                if name.startswith("mask"):
                    pe.wait_ge(side_by_act, by_act("gate_onehot", n))
                    last = nc.tensor.matmul(side[:, :], choose_sb[:, e, :], onehotT[:, :], start=True, stop=True)
                if name == "expert_back":
                    pe.wait_ge(e_emptied, n + 1)
                    last = turned(side, lambda t: backT[:, 1, 128 * t:128 * t + 128], ident_sb[:, :])
                last.then_inc(side_filled, 1)

            def pass_a(g, k):
                b, pair = divmod(g, PAIRS)
                if pair == 0 and k == 0:
                    pe.wait_ge(stacked[b % 2], 16 * 24 * (b // 2 + 1))
                    pe.wait_ge(loaded_rows, 16 * 16)
                for par in range(2):
                    n = 6 * g + 2 * k + par
                    if n >= AB:
                        pe.wait_ge(a_emptied, n - AB + 1)
                    rows = slice(64 * par, 64 * par + R_MAX)
                    for t, keys, at in ASTEP[k]:
                        q0 = pair * T + 128 * t
                        last = nc.tensor.matmul(a_bank[n % AB][:, at:at + keys], q_stack[b % 2][rows, q0:q0 + 128],
                                                k_stack[b % 2][rows, pair * T:pair * T + keys], start=True, stop=True)
                    last.then_inc(a_filled, 1)

            def pass_b(g, k):
                b, pair = divmod(g, PAIRS)
                if k == 0 and g % 2 == 0:
                    pe.wait_ge(max_rows[g // 2 % 2], 64 * (g // 4 + 1))
                for par in range(2):
                    n = 6 * g + 2 * k + par
                    if n >= BB:
                        pe.wait_ge(b_emptied, n - BB + 1)
                    rows = slice(64 * par, 64 * par + (R_END if k == 0 else R_MASK))
                    for kt, qt, cols, at in BSTEP[k]:
                        q0, k0 = pair * T + 128 * qt, pair * T + 128 * kt
                        last = nc.tensor.matmul(b_bank[n % BB][:, at:at + cols], k_stack[b % 2][rows, k0:k0 + 128],
                                                q_stack[b % 2][rows, q0:q0 + cols], start=True, stop=True)
                    last.then_inc(b_filled, 1)

            def values(u):
                b, quad = divmod(u, QUADS)
                pe.wait_ge(b_emptied, 12 * (u + 1))
                pe.wait_ge(zeroed, 4 * (u + 1))
                pe.wait_ge(side_by_act, by_act("value", b))
                if u >= 1:
                    pe.wait_ge(v_emptied, u)
                for s in range(3):
                    for kt, qt, cols, at in BSTEP[s]:
                        for c in range(4):
                            last = nc.tensor.matmul(v_bank[32 * c:32 * c + 32, 128 * qt:128 * qt + cols],
                                                    v_aug[:, b % 2, kt, 4 * quad + c, :],
                                                    probs[:, u % 2, c, P_AT[s] + at:P_AT[s] + at + cols],
                                                    start=(s == 0 and kt == 0), stop=(s == 2),
                                                    tile_position=(0, 32 * c))
                last.then_inc(v_filled, 1)

            pe.wait_ge(loaded_w, LOADED_W)
            pe.wait_ge(silu_done, 1)
            for j in range(6):
                last = nc.tensor.matmul(e_bank[:, B * j:B * j + B], wmod_sb[:, D * j:D * j + D], c_silu[:, :],
                                        start=True, stop=True)
            last.then_inc(mod_summed, 1)
            for g, k in PLACES:
                here = tasks(g, k)
                if 0 <= g < NP:
                    pass_a(g, k)
                if k == 1 and g % 2 == 1 and 0 <= (g - 5) // 2 < NP // 2:
                    values((g - 5) // 2)
                if 0 <= g - LAG < NP:
                    pass_b(g - LAG, k)
                for name, n in here:
                    task(name, n)
                    if name == f"mask{E - 1}":
                        feed_expert(E - 1, n)

        @block.scalar
        def _(act):
            def task(name, n):
                if name in BY_DVE:
                    return
                act.wait_ge(side_filled, USE[name, n] + 1)
                if name == "norm1":
                    if n == 0:
                        act.wait_ge(mod_ready, 1)
                    ins = nc.scalar.activation(hT[:, :], side[:, :], ACT.Identity, bias=mod_sb[:, 0, n:n + 1],
                                               scale=mod_sb[:, 1, n:n + 1])
                if name in ("query", "key"):
                    s = int(name == "key")
                    if n >= 1:
                        act.wait_ge(parts_done, 2 * (n - 1) + s + 1)
                    ins = nc.scalar.activation(proj[:, s, :], side[:, :], ACT.Copy,
                                               scale=1.0 if s else float(DH) ** -0.5)
                if name == "value":
                    act.wait_ge(v_cleared, 2)
                    if n >= 2:
                        act.wait_ge(v_filled, QUADS * (n - 1))
                    ins = nc.scalar.activation(v_aug[:, n % 2, :, :, 0:DH],
                                               side[:, :].rearrange("p (t h d) -> p t h d", t=TT, h=H), ACT.Copy)
                if name == "maxima":
                    if n >= 2:
                        act.wait_ge(max_rows[n % 2], 64 * (n // 2))
                    ins = nc.scalar.activation(maxT[:, n % 2, :], side[0:8, 0:256].bitcast(bf16), ACT.Copy)
                if name == "attn":
                    ins = nc.scalar.activation(attnT[:, :], side[:, :], ACT.Copy)
                if name == "outproj":
                    ins = nc.scalar.activation(backT[:, 0, :], side[:, :], ACT.Copy, scale=gates[:, 0, n:n + 1])
                if name == "norm2":
                    if n >= 1:
                        act.wait_ge(side_by_dve, by_dve(f"mask{E - 1}", n - 1))
                    ins = nc.scalar.activation(h2T[:, :], side[:, :], ACT.Identity, bias=mod_sb[:, 3, n:n + 1],
                                               scale=mod_sb[:, 4, n:n + 1])
                if name == "gate_onehot":
                    ins = nc.scalar.activation(onehotT[:, :], side[0:E, 0:256].bitcast(bf16), ACT.Copy)
                ins.then_inc(side_by_act, 1)

            def exps(g, k):
                u = g // 2
                for par in range(2):
                    n = 6 * g + 2 * k + par
                    act.wait_ge(b_filled, n + 1)
                    if u >= 2 and g % 2 == 0 and k == 0 and par == 0:
                        act.wait_ge(v_filled, u - 1)
                    nc.scalar.activation(probs[:, u % 2, 2 * (g % 2) + par, P_AT[k]:P_AT[k] + WIDTH[k]],
                                         b_bank[n % BB][:, 0:WIDTH[k]], ACT.Exp).then_inc(b_emptied, 1)

            act.wait_ge(loaded_c, 16)
            nc.scalar.activation(c_exp[:, :], c_sb[:, :], ACT.Exp, scale=-1.0).then_inc(silu_exp, 1)
            act.wait_ge(mod_summed, 1)
            nc.scalar.activation(mod_sb[:, :, :], e_bank[:, 0:6 * B].rearrange("p (j b) -> p j b", j=6), ACT.Copy)\
                .then_inc(mod_copied, 1)
            for g, k in PLACES:
                if 0 <= g - LAG < NP:
                    exps(g - LAG, k)
                if k == 1 and g % 2 == 1 and 0 <= (g - 5) // 2 < NP // 2:
                    u = (g - 5) // 2
                    act.wait_ge(v_filled, u + 1)
                    if u >= 1:
                        act.wait_ge(side_by_dve, by_dve("heads_back", u - 1))
                    nc.scalar.activation(headsT[:, :], v_bank[:, :], ACT.Copy).then_inc(v_emptied, 1)
                for name, n in tasks(g, k):
                    task(name, n)
                if (g % 8, k) == (4, 0) and 0 <= g // 8 - 2 < B:
                    b = g // 8 - 2
                    act.wait_ge(experts_fed, E * (b + 1))
                    nc.scalar.activation(backT[:, 1, :], e_bank[:, :], ACT.Copy, scale=gates[:, 1, b:b + 1])\
                        .then_inc(e_emptied, 1)

        @block.vector
        def _(dve):
            steps = [0]

            def link(ins):
                steps[0] += 1
                ins.then_inc(dve_step, 1)
                dve.wait_ge(dve_step, steps[0])

            def begin_norm(n, src):
                if n >= 1:
                    dve.wait_ge(norm_done, n)
                for t in range(TT):
                    last = nc.vector.bn_stats(stats[:, t, :], src[:, t, :])
                link(last)
                for t in range(TT):
                    last = nc.vector.bn_aggr(meanvar[:, t, :], stats[:, t, :])
                link(last)
                link(nc.vector.tensor_scalar(var_eps[:, :], meanvar[:, :, 1], EPS, None, ALU.add))
                link(nc.vector.tensor_scalar(half_bits[:, :], var_eps[:, :].bitcast(i32), 1, None,
                                             ALU.logical_shift_right))
                nc.vector.tensor_scalar(rstd[:, :].bitcast(i32), half_bits[:, :], -1.0, float(0x5F3759DF),
                                        ALU.mult, ALU.add).then_inc(rsqrt_begun, 1)

            def task(name, n):
                if name not in BY_DVE:
                    return
                dve.wait_ge(side_filled, USE[name, n] + 1)
                if name == "heads_back":
                    b, quad = divmod(n, QUADS)
                    if quad == 0 and b >= 1:
                        dve.wait_ge(side_by_act, by_act("attn", b - 1))
                    got = side[:, :].rearrange("p (t c w) -> p t c w", t=TT, c=4)
                    link(nc.vector.reciprocal(inv_sum[:, :, :], got[:, :, :, DH]))
                    dst = attn[:, :, 32 * quad:32 * quad + 32].rearrange("p t (c d) -> p t c d", c=4)
                    nc.vector.tensor_tensor(dst, got[:, :, :, 0:DH],
                                            inv_sum[:, :, :].unsqueeze(3).broadcast_to([128, TT, 4, DH]),
                                            ALU.mult).then_inc(side_by_dve, 1)
                if name == "attn_back":
                    nc.vector.tensor_tensor(x1[:, n % 2, :, :], side[:, :].rearrange("p (t d) -> p t d", t=TT),
                                            x_sb[:, n, :, :], ALU.add).then_inc(side_by_dve, 1)
                if name == "gate":
                    got = side[:, 0:TT * E].rearrange("p (t e) -> p t e", t=TT)
                    link(nc.vector.reduce_max(top[:, :], got, AX.X))
                    nc.vector.tensor_tensor(is_top[:, :, :], got, top[:, :].unsqueeze(2).broadcast_to([128, TT, E]),
                                            ALU.is_equal).then_inc(side_by_dve, 1)
                    dve.wait_ge(side_by_dve, by_dve(name, n))
                    link(nc.vector.tensor_tensor(rank[:, :, :], is_top[:, :, :],
                                                 order_sb[:, :].unsqueeze(1).broadcast_to([128, TT, E]), ALU.mult))
                    link(nc.vector.reduce_max(top[:, :], rank[:, :, :], AX.X))
                    nc.vector.tensor_tensor(onehot[:, :, :], rank[:, :, :],
                                            top[:, :].unsqueeze(2).broadcast_to([128, TT, E]), ALU.is_equal)\
                        .then_inc(onehot_ready, 1)
                if name.startswith("mask"):
                    e = int(name[4:])
                    if E * n + e >= 2:
                        dve.wait_ge(experts_fed, E * n + e - 1)
                    nc.vector.tensor_tensor(masked[:, e % 2, :], side[:, :], h2T[:, :], ALU.mult)\
                        .then_inc(side_by_dve, 1)
                if name == "expert_back":
                    if n >= 1:
                        dve.wait_ge(stored, 16 * n)
                    nc.vector.tensor_tensor(result[:, :, :], side[:, :].rearrange("p (t d) -> p t d", t=TT),
                                            x1[:, n % 2, :, :], ALU.add).then_inc(side_by_dve, 1)

            def pass_a_max(g, k):
                u = g // 2
                for par in range(2):
                    n = 6 * g + 2 * k + par
                    c = 2 * (g % 2) + par
                    if n >= 4:
                        dve.wait_ge(a_emptied, n - 3)
                    dve.wait_ge(a_filled, n + 1)
                    for t, keys, at in ASTEP[k]:
                        last = nc.vector.tensor_tensor_reduce(
                            out=scored[:, n % 4, at:at + keys], in0=a_bank[n % AB][:, at:at + keys], in1=causal_sb[:, T - keys:T],
                            scale=1.0, scalar=-3.0e38, op0=ALU.add, op1=ALU.max,
                            accum_out=maxima[:, u % 2, t, c:c + 1])
                    last.then_inc(a_emptied, 1)
                if g % 2 == 1 and k == 2:
                    dve.wait_ge(a_emptied, 6 * (g + 1))
                    if u >= 2:
                        dve.wait_ge(side_filled, USE["maxima", u - 2] + 1)
                    hi, lo = neg_max[:, u % 2, :, :, 0], neg_max[:, u % 2, :, :, 1]
                    link(nc.vector.tensor_scalar(hi, maxima[:, u % 2, :, :], -1.0, None, ALU.mult))
                    nc.vector.scalar_tensor_tensor(out=lo, in0=maxima[:, u % 2, :, :], scalar=-1.0, in1=hi,
                                                   op0=ALU.mult, op1=ALU.subtract).then_inc(maxima_split, 1)

            dve.wait_ge(loaded_x, 16 * TT)
            begin_norm(0, x_sb[:, 0, :, :])
            dve.wait_ge(silu_exp, 1)
            link(nc.vector.tensor_scalar(c_exp[:, :], c_exp[:, :], 1.0, None, ALU.add))
            link(nc.vector.reciprocal(c_exp[:, :], c_exp[:, :]))
            nc.vector.tensor_tensor(c_silu[:, :], c_exp[:, :], c_sb[:, :], ALU.mult).then_inc(silu_done, 1)
            dve.wait_ge(mod_copied, 1)
            for i in range(2):
                nc.vector.tensor_scalar(gate_sign[:, i, :], mod_sb[:, 3 * i + 2, :], 0.0, 2.0, ALU.is_ge, ALU.mult)
                link(nc.vector.tensor_scalar(gate_size[:, i, :], mod_sb[:, 3 * i + 2, :], -1.0, None, ALU.mult))
                link(nc.vector.tensor_tensor(gate_size[:, i, :], gate_size[:, i, :], mod_sb[:, 3 * i + 2, :], ALU.max))
                link(nc.vector.tensor_scalar(gate_size[:, i, :], gate_size[:, i, :], 0.25, None, ALU.max))
                link(nc.vector.scalar_tensor_tensor(out=gates[:, i, :], in0=gate_sign[:, i, :], scalar=-1.0,
                                                    in1=gate_size[:, i, :], op0=ALU.add, op1=ALU.mult))
                last = nc.vector.tensor_scalar(mod_sb[:, 3 * i + 1, :], mod_sb[:, 3 * i + 1, :], 1.0, None, ALU.add)
            last.then_inc(mod_ready, 1)
            dve.wait_ge(loaded_w, LOADED_W)
            norms = 1
            for g, k in PLACES:
                if 0 <= g < NP:
                    pass_a_max(g, k)
                for name, n in tasks(g, k):
                    task(name, n)
                    if name == "attn_back":
                        dve.wait_ge(side_by_dve, by_dve(name, n))
                        begin_norm(norms, x1[:, n % 2, :, :])
                        norms += 1
                if g >= 0 and g % 8 == 0 and k == 0 and g // 8 + 1 < B:
                    begin_norm(norms, x_sb[:, g // 8 + 1, :, :])
                    norms += 1


def constants(B=4, T=512, H=16, E=8):
    import numpy as np

    def bf(v):
        return np.asarray(v).astype(np.dtype("bfloat16"))

    PAIRS = H // 2
    pos = bf(np.arange(T) - T // 2)
    block = np.arange(T) % 128 // 16
    qrows = bf(np.zeros((2, 13, PAIRS, T)))
    krows = bf(np.zeros((2, 15, PAIRS, T)))
    for par in range(2):
        for pair in range(PAIRS):
            left = np.float32(2.0 ** (-8.0 * (2 * pair + par + 1) / H))
            for n in range(3):
                part = bf(left)
                left = np.float32(left - np.float32(part))
                qrows[par, 2 * n, pair] = part
                qrows[par, 2 * n + 1, pair] = pos
                krows[par, 2 * n, pair] = pos
                krows[par, 2 * n + 1, pair] = -part
    krows[:, 6:8] = 1.0
    for s in range(1, 8):
        qrows[:, 5 + s, :, :] = bf(block < s)
        krows[:, 7 + s, :, :] = bf(np.where(block == s, -16384.0, 0.0))
    causal = np.zeros((128, T), np.float32)
    causal[:, T - 128:] = np.where(np.arange(128)[None, :] > np.arange(128)[:, None], -1e30, 0.0)
    choose = bf(np.zeros((E, E, 128)))
    for e in range(E):
        choose[e, e, :] = 1.0
    return {"qrows": qrows.reshape(2, 13, -1), "krows": krows.reshape(2, 15, -1),
            "ident": np.eye(128, dtype=np.float32), "identb": bf(np.eye(128)), "causal": causal,
            "choose": choose, "order": np.tile(np.arange(E, 0, -1, dtype=np.float32), (128, 1))}


def kernel(L0_attn_x, L0_attn_Wq, L0_attn_Wk, L0_attn_Wv, L0_attn_Wo, L0_ffn_gate_w, L0_ffn_expert_w, L0_c, L0_wmod):
    import numpy as np
    import concourse.bacc as bacc
    from concourse import mybir as mb
    from concourse.bass_utils import run_bass_kernel_spmd

    feature = np.array([(2 * pair + par) * 8 + d for par in range(2) for d in range(8) for pair in range(8)])
    arrays = {
        "x": L0_attn_x,
        "wqT": L0_attn_Wq[feature].T,
        "wkT": L0_attn_Wk[feature].T,
        "wvT": L0_attn_Wv.T,
        "woT": L0_attn_Wo.T,
        "gwT": L0_ffn_gate_w.T,
        "ewT": L0_ffn_expert_w.transpose(2, 0, 1),
        "cT": L0_c.T,
        "wmod": L0_wmod,
    }
    arrays = {k: np.ascontiguousarray(v) for k, v in {**arrays, **constants()}.items()}
    nc = bacc.Bacc("TRN2", target_bir_lowering=False, num_devices=1)
    args = [nc.dram_tensor(k, a.shape, mb.dt.from_np(a.dtype), kind="ExternalInput").ap() for k, a in arrays.items()]
    out = nc.dram_tensor("out", L0_attn_x.shape, mb.dt.float32, kind="ExternalOutput").ap()
    adaln_block(nc, *args, out)
    r = run_bass_kernel_spmd(nc, [arrays], core_ids=[0])
    return r.results[0]["out"]
```

```python
import concourse.bass as bass
from concourse import mybir
from contextlib import ExitStack


def adaln_block(nc, x, wqT, wkT, wvT, woT, gwT, ewT, cT, wmod, qbias, kbias, kones, qmask, kmask, ident, identb, causal,
                order, out):
    f32, bf16, i32 = mybir.dt.float32, mybir.dt.bfloat16, mybir.dt.int32
    ALU, ACT, AX = mybir.AluOpType, mybir.ActivationFunctionType, mybir.AxisListType

    B, T, D = x.shape
    H = 16
    DH = D // H
    E = gwT.shape[1]
    TT = T // 128
    PAIRS = H // 2
    QUADS = H // 4
    NP = B * PAIRS
    EPS = 1e-5
    R_PROD, R_HEAD = 6, 54
    R_MAX = 2 * R_HEAD
    R_MASK = R_MAX + 4
    R_END = R_MASK + 7
    QPART = [0, 1, 2, 0, 1, 0]
    KPART = [2, 1, 0, 1, 0, 0]
    RUNS = [(0, 3), (3, 2), (5, 1)]
    LAG = 4
    AB, BB = 3, 2
    PW = 1280
    BSTEP = [[(t, t, 128, 128 * t) for t in range(TT)],
             [(0, 1, 384, 0), (2, 3, 128, 384)],
             [(1, 2, 256, 0)]]
    ASTEP = [[(3, 512, 0)], [(2, 384, 0), (0, 128, 384)], [(1, 256, 0)]]
    WIDTH = [512, 512, 256]
    P_AT = [0, 512, 1024]

    SIDE = {(0, 0): [("norm2", 2)], (0, 2): [("gate", 2)], (1, 2): [("gate_onehot", 2)],
            (2, 0): [("norm1", -1)], (2, 2): [("query", -1)], (3, 2): [("key", -1)], (4, 2): [("value", -1)],
            (5, 2): [("attn", 1)], (6, 0): [("outproj", 1)], (6, 2): [("attn_back", 1)],
            (7, 0): [("expert_back", 2)]}
    FEED = {(3, 0): 0, (3, 1): 1, (3, 2): 2, (4, 0): 3, (4, 1): 4, (4, 2): 5, (5, 0): 6, (5, 1): 7}
    BY_POOL = [1, 4, 7]
    STORE, FETCH = {(3, 2): 0, (4, 2): 1}, {(4, 0): 0, (5, 0): 1}
    LAST = 8 * (B + 1) + 7 + 1
    VALUES = [[(0, 0, 128, 0), (1, 1, 128, 128)], [(2, 2, 128, 256), (3, 3, 128, 384)],
              [(0, 1, 256, 512)], [(0, 3, 128, 768), (2, 3, 128, 896)], [(1, 2, 256, 1024)]]

    def value_step(g, k):
        u, step = divmod(3 * (g - 5) + k - 2, 6)
        return (u, step) if 0 <= u < NP // 2 and step < len(VALUES) else None

    def feed(g, k, early=0):
        g, k = divmod(3 * g + k + early, 3)
        e, b = FEED.get((g % 8, k)), g // 8 - 2
        return (b, e) if e is not None and 0 <= b < B else None

    def tasks(g, k):
        found = []
        if g < 0:
            return [(name, 0) for name in ("norm1", "query", "key", "value")] if k == 0 else []
        if g % 2 == 1 and k == 1 and 0 <= (g - 7) // 2 < NP // 2:
            found.append(("heads_back", (g - 7) // 2))
        if g % 2 == 0 and k == 1 and 0 <= g // 2 - 1 < NP // 2:
            found.append(("maxima", g // 2 - 1))
        for name, ahead in SIDE.get((g % 8, k), []):
            b = g // 8 - ahead
            if 0 <= b < B and not (ahead == -1 and b == 0):
                found.append((name, b))
        return found

    PLACES = [(-1, 0)] + [(g, k) for g in range(LAST) for k in range(3)]
    BY_DVE = {"heads_back", "attn_back", "gate", "expert_back"}
    USES = [t for p in PLACES for t in tasks(*p)]
    USE = {t: n for n, t in enumerate(USES)}

    def emptied(n):
        dve = sum(name in BY_DVE for name, _ in USES[:n])
        return dve, n - dve

    def by_dve(name, n):
        return emptied(USE[name, n] + 1)[0]

    def by_act(name, n):
        return emptied(USE[name, n] + 1)[1]

    NORMS = [("norm1", 0)]
    for g in range(LAST):
        for k in range(3):
            if g % 8 == 0 and k == 1 and g // 8 + 1 < B:
                NORMS.append(("norm1", g // 8 + 1))
            NORMS += [("norm2", b) for name, b in tasks(g, k) if name == "attn_back"]

    ctx = ExitStack()
    with ctx:
        def sb(name, shape, dt=f32):
            return ctx.enter_context(nc.sbuf_tensor(name, shape, dt))

        def pb(name):
            return ctx.enter_context(nc.psum_tensor(name, [128, 512], f32))

        def sem(name):
            return ctx.enter_context(nc.semaphore(name))

        wq_sb, wk_sb, wv_sb, wo_sb = (sb(n, [D, D]) for n in ("wq_sb", "wk_sb", "wv_sb", "wo_sb"))
        gw_sb = sb("gw_sb", [D, E])
        ew_in = sb("ew_in", [D, E, D])
        ew_sb = sb("ew_sb", [D, E, D])
        wmod_sb = sb("wmod_sb", [D, 6 * D])
        ident_sb = sb("ident_sb", [128, 128])
        identb_sb = sb("identb_sb", [128, 128], bf16)
        causal_sb = sb("causal_sb", [128, 512])
        order_sb = sb("order_sb", [128, E])
        c_sb, c_exp, c_silu = sb("c_sb", [D, B]), sb("c_exp", [D, B]), sb("c_silu", [D, B])
        mod_sb = sb("mod_sb", [D, 6, B])
        gates = sb("gates", [D, 2, B])
        gate_sign, gate_size = sb("gate_sign", [D, 2, B]), sb("gate_size", [D, 2, B])
        x_sb = sb("x_sb", [128, B, TT, D])
        stats = sb("stats", [128, TT, 6])
        meanvar = sb("meanvar", [128, TT, 2])
        var_eps = sb("var_eps", [128, TT])
        half_bits = sb("half_bits", [128, TT], i32)
        rstd = sb("rstd", [128, TT])
        newton = sb("newton", [128, TT])
        normed = sb("normed", [128, TT, D])
        hT = sb("hT", [D, T])
        proj = sb("proj", [128, 2, T])
        rest = sb("rest", [128, 2, T])
        parts = sb("parts", [128, 2, 3, T], bf16)
        q_stack = [sb(f"q_stack{i}", [128, PAIRS * T], bf16) for i in range(2)]
        k_stack = [sb(f"k_stack{i}", [128, 2 * PAIRS * T], bf16) for i in range(2)]
        v_aug = sb("v_aug", [128, 2, TT, H, 32])
        scored = sb("scored", [128, 4, 512], bf16)
        maxima = sb("maxima", [128, 2, TT, 4])
        neg_max = sb("neg_max", [128, 2, TT, 4, 2], bf16)
        maxT = sb("maxT", [8, 2, T], bf16)
        probs = sb("probs", [128, 2, 4, PW])
        headsT = sb("headsT", [128, T])
        inv_sum = sb("inv_sum", [128, TT, 4])
        attn = sb("attn", [128, TT, D])
        attnT = sb("attnT", [D, T])
        backT = sb("backT", [D, 2, T])
        x1 = sb("x1", [128, 2, TT, D])
        h2T = sb("h2T", [D, T])
        top = sb("top", [128, TT])
        is_top = sb("is_top", [128, TT, E])
        rank = sb("rank", [128, TT, E])
        onehot = sb("onehot", [128, TT, E], bf16)
        onehotT = sb("onehotT", [E, T], bf16)
        chosen = sb("chosen", [128, E, T], bf16)
        masked = sb("masked", [D, 4, T])
        result = sb("result", [128, TT, D])
        scratch = nc.dram_tensor("parts_scratch", [B, 2, 2, 3, 64, T], bf16).ap()
        onehot_dram = nc.dram_tensor("onehot_scratch", [B, E, T], bf16).ap()

        a_bank = [pb(f"a_bank{i}") for i in range(AB)]
        b_bank = [pb(f"b_bank{i}") for i in range(BB)]
        v_bank = pb("v_bank")
        e_bank = pb("e_bank")
        side = pb("side")

        loaded_x = sem("loaded_x")
        loaded_c = sem("loaded_c")
        loaded_mod = sem("loaded_mod")
        loaded_attn = sem("loaded_attn")
        loaded_causal = sem("loaded_causal")
        loaded_w = sem("loaded_w")
        loaded_rows = [sem(f"loaded_rows{i}") for i in range(2)]
        v_cleared = sem("v_cleared")
        k_cleared = [sem(f"k_cleared{i}") for i in range(2)]
        experts_ready = sem("experts_ready")
        silu_exp = sem("silu_exp")
        silu_done = sem("silu_done")
        mod_summed = sem("mod_summed")
        mod_copied = sem("mod_copied")
        mod_ready = sem("mod_ready")
        rsqrt_begun = sem("rsqrt_begun")
        rstd_ready = sem("rstd_ready")
        norm_done = sem("norm_done")
        side_filled = sem("side_filled")
        side_by_dve = sem("side_by_dve")
        side_by_act = sem("side_by_act")
        parts_done = [sem(f"parts_done{i}") for i in range(2)]
        parts_stored = [sem(f"parts_stored{i}") for i in range(2)]
        stacked = [sem(f"stacked{i}") for i in range(2)]
        a_filled = sem("a_filled")
        a_emptied = sem("a_emptied")
        b_filled = sem("b_filled")
        b_emptied = sem("b_emptied")
        maxima_split = sem("maxima_split")
        max_rows = [sem(f"max_rows{i}") for i in range(2)]
        zeroed = sem("zeroed")
        v_filled = sem("v_filled")
        v_emptied = sem("v_emptied")
        onehot_ready = sem("onehot_ready")
        onehot_stored = sem("onehot_stored")
        chosen_ready = sem("chosen_ready")
        masked_by_dve = sem("masked_by_dve")
        masked_by_pool = sem("masked_by_pool")
        experts_fed = sem("experts_fed")
        e_emptied = sem("e_emptied")
        stored = sem("stored")
        dve_step = sem("dve_step")
        pool_step = sem("pool_step")

        LOADED_ATTN, LOADED_W = 16 * 4, 16 * 6
        block = ctx.enter_context(nc.Block())

        def masked_count(b, e):
            mine = [i for i in range(E) if (i in BY_POOL) == (e in BY_POOL)]
            n = len(mine) * b + mine.index(e)
            return (masked_by_pool if e in BY_POOL else masked_by_dve), n + 1, n % 2 + 2 * (e in BY_POOL)

        def fed_before(b, e):
            mine = [i for i in range(E) if (i in BY_POOL) == (e in BY_POOL)]
            n = len(mine) * b + mine.index(e) - 2
            return 0 if n < 0 else E * (n // len(mine)) + mine[n % len(mine)] + 1

        @block.sync
        def _(sp):
            sp.dma_start(x_sb[:, 0, :, :], x[0].rearrange("(t p) d -> p t d", p=128)).then_inc(loaded_x, 16)
            sp.dma_start(c_sb[:, :], cT).then_inc(loaded_c, 16)
            sp.dma_start(wmod_sb[:, :], wmod).then_inc(loaded_mod, 16)
            for dst, src in ((ident_sb[:, :], ident), (wq_sb[:, :], wqT), (wk_sb[:, :], wkT), (wv_sb[:, :], wvT)):
                sp.dma_start(dst, src).then_inc(loaded_attn, 16)

            def rows(i):
                sp.wait_ge(k_cleared[i], 1)
                W = PAIRS * T
                for par in range(2):
                    at = R_HEAD * par
                    sp.dma_start(q_stack[i][at:at + R_PROD, :], qbias[par]).then_inc(loaded_rows[i], 16)
                    sp.dma_start(k_stack[i][at:at + R_PROD, W * par:W * par + W], kbias[par])\
                      .then_inc(loaded_rows[i], 16)
                    at = R_MAX + 2 * par
                    sp.dma_start(k_stack[i][at:at + 2, W * par:W * par + W], kones).then_inc(loaded_rows[i], 16)
                sp.dma_start(q_stack[i][R_MASK:R_END, :], qmask).then_inc(loaded_rows[i], 16)
                sp.dma_start(k_stack[i][R_MASK:R_END, :], kmask).then_inc(loaded_rows[i], 16)

            def store_parts(b, s):
                sp.wait_ge(parts_done[s], b + 1)
                for par in range(2):
                    sp.dma_start(scratch[b, s, par].rearrange("n p t -> p n t"),
                                 parts[64 * par:64 * par + 64, s, :, :]).then_inc(parts_stored[s], 16)

            def fetch_parts(b, s):
                st = (q_stack if s == 0 else k_stack)[b % 2]
                if b >= 2:
                    sp.wait_ge(b_filled, 3 * PAIRS * 2 * (b - 1))
                sp.wait_ge(parts_stored[s], 32 * (b + 1))
                for first, n in RUNS:
                    for par in range(2):
                        at = R_HEAD * par + R_PROD + DH * first
                        cols = slice(PAIRS * T * par, PAIRS * T * (par + 1)) if s else slice(0, PAIRS * T)
                        have = (2 - KPART[first]) if s else QPART[first]
                        src = scratch[b, s, par, have:have + n]
                        sp.dma_start(st[at:at + DH * n, cols], src.rearrange("n (d j) t -> (n d) (j t)", d=DH))\
                          .then_inc(stacked[b % 2], 16)

            sp.dma_start(causal_sb[:, :], causal).then_inc(loaded_causal, 16)
            rows(0)
            store_parts(0, 0)
            fetch_parts(0, 0)
            store_parts(0, 1)
            fetch_parts(0, 1)
            for dst, src in ((identb_sb[:, :], identb), (ew_in[:, :, :], ewT), (wo_sb[:, :], woT),
                             (gw_sb[:, :], gwT), (order_sb[:, :], order),
                             (x_sb[:, 1:B, :, :], x[1:B].rearrange("b (t p) d -> p b t d", p=128))):
                sp.dma_start(dst, src).then_inc(loaded_w, 16)
            rows(1)

            for g, k in PLACES:
                if 0 <= g // 8 + 1 < B and g >= 0:
                    if (g % 8, k) in STORE:
                        store_parts(g // 8 + 1, STORE[g % 8, k])
                    if (g % 8, k) in FETCH:
                        fetch_parts(g // 8 + 1, FETCH[g % 8, k])
                if (g % 8, k) == (2, 0) and 0 <= g // 8 - 2 < B:
                    n = g // 8 - 2
                    sp.wait_ge(onehot_stored, 16 * (n + 1))
                    if n >= 1:
                        sp.wait_ge(masked_by_dve, masked_count(n - 1, 6)[1])
                        sp.wait_ge(masked_by_pool, masked_count(n - 1, 7)[1])
                    sp.dma_start(chosen[:, :, :], onehot_dram[n].rearrange("e t -> (e t)").partition_broadcast(128))\
                      .then_inc(chosen_ready, 16)
                for name, n in tasks(g, k):
                    if name == "maxima":
                        sp.wait_ge(side_by_act, by_act(name, n))
                        for c in range(4):
                            pair = (4 * n + c) // 2 % PAIRS
                            at = R_MAX + 2 * (c % 2)
                            dst = q_stack[n // QUADS % 2][at:at + 2, pair * T:(pair + 1) * T]
                            sp.dma_start(dst, maxT[2 * c:2 * c + 2, n % 2, :]).then_inc(max_rows[n % 2], 16)
                    if name == "gate_onehot":
                        sp.wait_ge(side_by_act, by_act(name, n))
                        sp.dma_start(onehot_dram[n], onehotT[:, :]).then_inc(onehot_stored, 16)
                    if name == "expert_back":
                        sp.wait_ge(side_by_dve, by_dve(name, n))
                        sp.dma_start(out[n].rearrange("(t p) d -> p t d", p=128), result[:, :, :]).then_inc(stored, 16)
            sp.wait_ge(stored, 16 * B)

        @block.gpsimd
        def _(pool):
            steps = [0]

            def link(ins):
                steps[0] += 1
                ins.then_inc(pool_step, 1)
                pool.wait_ge(pool_step, steps[0])

            def newton_steps(n):
                pool.wait_ge(rsqrt_begun, n + 1)
                for step in range(3):
                    link(nc.gpsimd.tensor_tensor(newton[:, :], rstd[:, :], rstd[:, :], ALU.mult))
                    link(nc.gpsimd.tensor_tensor(newton[:, :], newton[:, :], var_eps[:, :], ALU.mult))
                    link(nc.gpsimd.tensor_scalar(newton[:, :], newton[:, :], -0.5, 1.5, ALU.mult, ALU.add))
                    last = nc.gpsimd.tensor_tensor(rstd[:, :], rstd[:, :], newton[:, :], ALU.mult)
                    if step < 2:
                        link(last)
                last.then_inc(rstd_ready, 1)

            def split(s, b):
                pool.wait_ge(side_by_act, by_act("key" if s else "query", b))
                part = [parts[:, s, 2 - n if s else n, :] for n in range(3)]
                nc.gpsimd.tensor_tensor(part[1], proj[:, s, :], part[0], ALU.subtract)
                link(nc.gpsimd.tensor_tensor(rest[:, s, :], proj[:, s, :], part[0], ALU.subtract))
                nc.gpsimd.tensor_tensor(part[2], rest[:, s, :], part[1], ALU.subtract).then_inc(parts_done[s], 1)

            nc.gpsimd.memset(k_stack[0][:, :].bitcast(f32), 0.0).then_inc(k_cleared[0], 1)
            norms = 0
            newton_steps(norms)
            norms += 1
            split(0, 0)
            nc.gpsimd.memset(k_stack[1][:, :].bitcast(f32), 0.0).then_inc(k_cleared[1], 1)
            nc.gpsimd.memset(v_aug[:, :, :, :, :], 0.0).then_inc(v_cleared, 1)
            pool.wait_ge(v_cleared, 1)
            nc.gpsimd.memset(v_aug[:, :, :, :, DH:DH + 1], 1.0).then_inc(v_cleared, 1)
            pool.wait_ge(loaded_w, LOADED_W)
            pool.wait_ge(loaded_attn, LOADED_ATTN)
            nc.gpsimd.tensor_tensor(ew_sb[:, :, :], ew_in[:, :, :],
                                    ident_sb[:, :].unsqueeze(1).broadcast_to([128, E, 128]), ALU.add)\
                .then_inc(experts_ready, 1)
            for g in range(LAST):
                for k in range(3):
                    if k == 0 and 0 <= g - LAG < NP:
                        pair = g - LAG
                        for par in range(2):
                            pool.wait_ge(b_emptied, 6 * pair + par + 1)
                            diag = probs[:, pair // 2 % 2, 2 * (pair % 2) + par, 0:512]\
                                .rearrange("p (t q) -> p t q", t=TT)
                            nc.gpsimd.affine_select(out=diag, in_=diag, compare_op=ALU.is_ge, fill=0.0, base=0,
                                                    pattern=[[0, TT], [1, 128]], channel_multiplier=-1)\
                                .then_inc(zeroed, 1)
                    if g % 8 == 0 and k == 1 and g // 8 + 1 < B:
                        newton_steps(norms)
                        norms += 1
                    if feed(g, k, 1) and feed(g, k, 1)[1] in BY_POOL:
                        b, e = feed(g, k, 1)
                        count, value, at = masked_count(b, e)
                        pool.wait_ge(chosen_ready, 16 * (b + 1))
                        pool.wait_ge(side_by_act, by_act("norm2", b))
                        if fed_before(b, e):
                            pool.wait_ge(experts_fed, fed_before(b, e))
                        nc.gpsimd.tensor_tensor(masked[:, at, :], h2T[:, :], chosen[:, e, :], ALU.mult)\
                            .then_inc(masked_by_pool, 1)
                    for name, b in tasks(g, k):
                        if name == "query":
                            split(0, b)
                        if name == "key":
                            split(1, b)
                        if name == "attn_back":
                            newton_steps(norms)
                            norms += 1

        @block.tensor
        def _(pe):
            def fill(task):
                dve, act = emptied(USE[task])
                if dve:
                    pe.wait_ge(side_by_dve, dve)
                if act:
                    pe.wait_ge(side_by_act, act)

            def turned(dst, src, idn, n=TT):
                for t in range(n):
                    last = nc.tensor.transpose(dst[:, 128 * t:128 * t + 128], src(t), idn)
                return last

            def feed_expert(e, b):
                count, value, at = masked_count(b, e)
                pe.wait_ge(count, value)
                if e == 0:
                    pe.wait_ge(experts_ready, 1)
                    if b >= 1:
                        pe.wait_ge(e_emptied, b)
                nc.tensor.matmul(e_bank[:, :], ew_sb[:, e, :], masked[:, at, :], start=(e == 0),
                                 stop=(e == E - 1)).then_inc(experts_fed, 1)

            def task(name, n):
                fill((name, n))
                if (name, n) == ("gate", 0) or (name, n) == ("maxima", 0):
                    pe.wait_ge(loaded_w, LOADED_W)
                if name == "norm1" or name == "norm2":
                    pe.wait_ge(norm_done, NORMS.index((name, n)) + 1)
                    last = turned(side, lambda t: normed[:, t, :], ident_sb[:, :])
                if name in ("query", "key", "value"):
                    pe.wait_ge(side_by_act, by_act("norm1", n))
                if name == "query":
                    last = nc.tensor.matmul(side[:, :], wq_sb[:, :], hT[:, :], start=True, stop=True)
                if name == "key":
                    last = nc.tensor.matmul(side[:, :], wk_sb[:, :], hT[:, :], start=True, stop=True)
                if name == "value":
                    for t in range(TT):
                        last = nc.tensor.matmul(side[:, 128 * t:128 * t + 128], hT[:, 128 * t:128 * t + 128],
                                                wv_sb[:, :], start=True, stop=True)
                if name == "maxima":
                    pe.wait_ge(maxima_split, n + 1)
                    last = turned(side[0:8, 0:256].bitcast(bf16),
                                  lambda t: neg_max[:, n % 2, t, :, :].rearrange("p c s -> p (c s)"), identb_sb[:, :])
                if name == "heads_back":
                    pe.wait_ge(v_emptied, n + 1)
                    last = turned(side, lambda t: headsT[:, 128 * t:128 * t + 128], ident_sb[:, :])
                if name == "attn":
                    pe.wait_ge(side_by_dve, by_dve("heads_back", QUADS * n + QUADS - 1))
                    last = turned(side, lambda t: attn[:, t, :], ident_sb[:, :])
                if name == "outproj":
                    pe.wait_ge(side_by_act, by_act("attn", n))
                    last = nc.tensor.matmul(side[:, :], wo_sb[:, :], attnT[:, :], start=True, stop=True)
                if name == "attn_back":
                    pe.wait_ge(side_by_act, by_act("outproj", n))
                    last = turned(side, lambda t: backT[:, 0, 128 * t:128 * t + 128], ident_sb[:, :])
                if name == "gate":
                    pe.wait_ge(side_by_act, by_act("norm2", n))
                    for t in range(TT):
                        last = nc.tensor.matmul(side[:, E * t:E * t + E], h2T[:, 128 * t:128 * t + 128],
                                                gw_sb[:, :], start=True, stop=True)
                if name == "gate_onehot":
                    pe.wait_ge(onehot_ready, n + 1)
                    last = turned(side[0:E, 0:256].bitcast(bf16), lambda t: onehot[:, t, :], identb_sb[:, :])
                if name == "expert_back":
                    pe.wait_ge(e_emptied, n + 1)
                    last = turned(side, lambda t: backT[:, 1, 128 * t:128 * t + 128], ident_sb[:, :])
                last.then_inc(side_filled, 1)

            def pass_a(g, k):
                b, pair = divmod(g, PAIRS)
                if pair == 0 and k == 0:
                    pe.wait_ge(stacked[b % 2], 16 * 12 * (b // 2 + 1))
                    pe.wait_ge(loaded_rows[b % 2], 16 * 8)
                for par in range(2):
                    n = 6 * g + 2 * k + par
                    if n >= AB:
                        pe.wait_ge(a_emptied, n - AB + 1)
                    k_at = (PAIRS * par + pair) * T
                    for t, keys, at in ASTEP[k]:
                        q0 = pair * T + 128 * t
                        last = nc.tensor.matmul(a_bank[n % AB][:, at:at + keys], q_stack[b % 2][0:R_MAX, q0:q0 + 128],
                                                k_stack[b % 2][0:R_MAX, k_at:k_at + keys], start=True, stop=True)
                    last.then_inc(a_filled, 1)

            def pass_b(g, k):
                b, pair = divmod(g, PAIRS)
                if k == 0 and g % 2 == 0:
                    pe.wait_ge(max_rows[g // 2 % 2], 64 * (g // 4 + 1))
                for par in range(2):
                    n = 6 * g + 2 * k + par
                    if n >= BB:
                        pe.wait_ge(b_emptied, n - BB + 1)
                    rows = slice(0, R_END if k == 0 else R_MASK)
                    for kt, qt, cols, at in BSTEP[k]:
                        q0, k0 = pair * T + 128 * qt, (PAIRS * par + pair) * T + 128 * kt
                        last = nc.tensor.matmul(b_bank[n % BB][:, at:at + cols], k_stack[b % 2][rows, k0:k0 + 128],
                                                q_stack[b % 2][rows, q0:q0 + cols], start=True, stop=True)
                    last.then_inc(b_filled, 1)

            def values(u, step):
                b, quad = divmod(u, QUADS)
                if step == 0:
                    pe.wait_ge(zeroed, 4 * (u + 1))
                    pe.wait_ge(side_by_act, by_act("value", b))
                    if u >= 1:
                        pe.wait_ge(v_emptied, u)
                if step == 2:
                    pe.wait_ge(b_emptied, 12 * (u + 1))
                for kt, qt, cols, at in VALUES[step]:
                    for c in range(4):
                        last = nc.tensor.matmul(v_bank[32 * c:32 * c + 32, 128 * qt:128 * qt + cols],
                                                v_aug[:, b % 2, kt, 4 * quad + c, :],
                                                probs[:, u % 2, c, at:at + cols],
                                                start=(step == 0 and kt == 0), stop=(step == len(VALUES) - 1),
                                                tile_position=(0, 32 * c))
                if step == len(VALUES) - 1:
                    last.then_inc(v_filled, 1)

            pe.wait_ge(loaded_mod, 16)
            pe.wait_ge(silu_done, 1)
            for j in range(6):
                last = nc.tensor.matmul(e_bank[:, B * j:B * j + B], wmod_sb[:, D * j:D * j + D], c_silu[:, :],
                                        start=True, stop=True)
            last.then_inc(mod_summed, 1)
            pe.wait_ge(loaded_attn, LOADED_ATTN)
            for g, k in PLACES:
                here = tasks(g, k)
                if 0 <= g < NP:
                    pass_a(g, k)
                if value_step(g, k):
                    values(*value_step(g, k))
                if 0 <= g - LAG < NP:
                    pass_b(g - LAG, k)
                for name, n in here:
                    task(name, n)
                if feed(g, k):
                    b, e = feed(g, k)
                    feed_expert(e, b)

        @block.scalar
        def _(act):
            def task(name, n):
                if name in BY_DVE:
                    return
                act.wait_ge(side_filled, USE[name, n] + 1)
                if name == "norm1":
                    if n == 0:
                        act.wait_ge(mod_ready, 1)
                    ins = nc.scalar.activation(hT[:, :], side[:, :], ACT.Identity, bias=mod_sb[:, 0, n:n + 1],
                                               scale=mod_sb[:, 1, n:n + 1])
                if name in ("query", "key"):
                    s = int(name == "key")
                    if n >= 1:
                        act.wait_ge(parts_done[s], n)
                        act.wait_ge(parts_stored[s], 32 * n)
                    scale = 1.0 if s else float(DH) ** -0.5
                    nc.scalar.activation(proj[:, s, :], side[:, :], ACT.Copy, scale=scale)
                    ins = nc.scalar.activation(parts[:, s, 2 if s else 0, :], side[:, :], ACT.Copy, scale=scale)
                if name == "value":
                    act.wait_ge(v_cleared, 2)
                    if n >= 2:
                        act.wait_ge(v_filled, QUADS * (n - 1))
                    ins = nc.scalar.activation(v_aug[:, n % 2, :, :, 0:DH],
                                               side[:, :].rearrange("p (t h d) -> p t h d", t=TT, h=H), ACT.Copy)
                if name == "maxima":
                    if n >= 2:
                        act.wait_ge(max_rows[n % 2], 64 * (n // 2))
                    ins = nc.scalar.activation(maxT[:, n % 2, :], side[0:8, 0:256].bitcast(bf16), ACT.Copy)
                if name == "attn":
                    ins = nc.scalar.activation(attnT[:, :], side[:, :], ACT.Copy)
                if name == "outproj":
                    ins = nc.scalar.activation(backT[:, 0, :], side[:, :], ACT.Copy, scale=gates[:, 0, n:n + 1])
                if name == "norm2":
                    if n >= 1:
                        act.wait_ge(experts_fed, E * n)
                    ins = nc.scalar.activation(h2T[:, :], side[:, :], ACT.Identity, bias=mod_sb[:, 3, n:n + 1],
                                               scale=mod_sb[:, 4, n:n + 1])
                if name == "gate_onehot":
                    if n >= 1:
                        act.wait_ge(onehot_stored, 16 * n)
                    ins = nc.scalar.activation(onehotT[:, :], side[0:E, 0:256].bitcast(bf16), ACT.Copy)
                ins.then_inc(side_by_act, 1)

            def exps(g, k):
                u = g // 2
                for par in range(2):
                    n = 6 * g + 2 * k + par
                    act.wait_ge(b_filled, n + 1)
                    if u >= 2 and g % 2 == 0 and k == 0 and par == 0:
                        act.wait_ge(v_filled, u - 1)
                    nc.scalar.activation(probs[:, u % 2, 2 * (g % 2) + par, P_AT[k]:P_AT[k] + WIDTH[k]],
                                         b_bank[n % BB][:, 0:WIDTH[k]], ACT.Exp).then_inc(b_emptied, 1)

            act.wait_ge(loaded_c, 16)
            nc.scalar.activation(c_exp[:, :], c_sb[:, :], ACT.Exp, scale=-1.0).then_inc(silu_exp, 1)
            act.wait_ge(mod_summed, 1)
            nc.scalar.activation(mod_sb[:, :, :], e_bank[:, 0:6 * B].rearrange("p (j b) -> p j b", j=6), ACT.Copy)\
                .then_inc(mod_copied, 1)
            for g, k in PLACES:
                if 0 <= g - LAG < NP:
                    exps(g - LAG, k)
                if value_step(g, k) and value_step(g, k)[1] == len(VALUES) - 1:
                    u = value_step(g, k)[0]
                    act.wait_ge(v_filled, u + 1)
                    if u >= 1:
                        act.wait_ge(side_by_dve, by_dve("heads_back", u - 1))
                    nc.scalar.activation(headsT[:, :], v_bank[:, :], ACT.Copy).then_inc(v_emptied, 1)
                for name, n in tasks(g, k):
                    task(name, n)
                if feed(g, k) and feed(g, k)[1] == E - 1:
                    b = feed(g, k)[0]
                    act.wait_ge(experts_fed, E * (b + 1))
                    nc.scalar.activation(backT[:, 1, :], e_bank[:, :], ACT.Copy, scale=gates[:, 1, b:b + 1])\
                        .then_inc(e_emptied, 1)

        @block.vector
        def _(dve):
            steps = [0]

            def link(ins):
                steps[0] += 1
                ins.then_inc(dve_step, 1)
                dve.wait_ge(dve_step, steps[0])

            def begin_norm(n, src):
                if n >= 1:
                    dve.wait_ge(norm_done, n)
                for t in range(TT):
                    last = nc.vector.bn_stats(stats[:, t, :], src[:, t, :])
                link(last)
                for t in range(TT):
                    last = nc.vector.bn_aggr(meanvar[:, t, :], stats[:, t, :])
                link(last)
                link(nc.vector.tensor_scalar(var_eps[:, :], meanvar[:, :, 1], EPS, None, ALU.add))
                link(nc.vector.tensor_scalar(half_bits[:, :], var_eps[:, :].bitcast(i32), 1, None,
                                             ALU.logical_shift_right))
                nc.vector.tensor_scalar(rstd[:, :].bitcast(i32), half_bits[:, :], -1.0, float(0x5F3759DF),
                                        ALU.mult, ALU.add).then_inc(rsqrt_begun, 1)

            def end_norm(n, src):
                dve.wait_ge(rstd_ready, n + 1)
                if n >= 1:
                    dve.wait_ge(side_filled, USE[NORMS[n - 1]] + 1)
                for t in range(TT):
                    last = nc.vector.tensor_scalar(normed[:, t, :], src[:, t, :], meanvar[:, t, 0:1],
                                                   rstd[:, t:t + 1], ALU.subtract, ALU.mult)
                last.then_inc(norm_done, 1)

            def task(name, n):
                if name not in BY_DVE:
                    return
                dve.wait_ge(side_filled, USE[name, n] + 1)
                if name == "heads_back":
                    b, quad = divmod(n, QUADS)
                    if quad == 0 and b >= 1:
                        dve.wait_ge(side_by_act, by_act("attn", b - 1))
                    got = side[:, :].rearrange("p (t c w) -> p t c w", t=TT, c=4)
                    link(nc.vector.reciprocal(inv_sum[:, :, :], got[:, :, :, DH]))
                    dst = attn[:, :, 32 * quad:32 * quad + 32].rearrange("p t (c d) -> p t c d", c=4)
                    nc.vector.tensor_tensor(dst, got[:, :, :, 0:DH],
                                            inv_sum[:, :, :].unsqueeze(3).broadcast_to([128, TT, 4, DH]),
                                            ALU.mult).then_inc(side_by_dve, 1)
                if name == "attn_back":
                    nc.vector.tensor_tensor(x1[:, n % 2, :, :], side[:, :].rearrange("p (t d) -> p t d", t=TT),
                                            x_sb[:, n, :, :], ALU.add).then_inc(side_by_dve, 1)
                if name == "gate":
                    got = side[:, 0:TT * E].rearrange("p (t e) -> p t e", t=TT)
                    link(nc.vector.reduce_max(top[:, :], got, AX.X))
                    nc.vector.tensor_tensor(is_top[:, :, :], got, top[:, :].unsqueeze(2).broadcast_to([128, TT, E]),
                                            ALU.is_equal).then_inc(side_by_dve, 1)
                    dve.wait_ge(side_by_dve, by_dve(name, n))
                    link(nc.vector.tensor_tensor(rank[:, :, :], is_top[:, :, :],
                                                 order_sb[:, :].unsqueeze(1).broadcast_to([128, TT, E]), ALU.mult))
                    link(nc.vector.reduce_max(top[:, :], rank[:, :, :], AX.X))
                    nc.vector.tensor_tensor(onehot[:, :, :], rank[:, :, :],
                                            top[:, :].unsqueeze(2).broadcast_to([128, TT, E]), ALU.is_equal)\
                        .then_inc(onehot_ready, 1)
                if name == "expert_back":
                    if n >= 1:
                        dve.wait_ge(stored, 16 * n)
                    nc.vector.tensor_tensor(result[:, :, :], side[:, :].rearrange("p (t d) -> p t d", t=TT),
                                            x1[:, n % 2, :, :], ALU.add).then_inc(side_by_dve, 1)

            def pass_a_max(g, k):
                u = g // 2
                for par in range(2):
                    n = 6 * g + 2 * k + par
                    c = 2 * (g % 2) + par
                    if n >= 4:
                        dve.wait_ge(a_emptied, n - 3)
                    dve.wait_ge(a_filled, n + 1)
                    for t, keys, at in ASTEP[k]:
                        last = nc.vector.tensor_tensor_reduce(
                            out=scored[:, n % 4, at:at + keys], in0=a_bank[n % AB][:, at:at + keys], in1=causal_sb[:, T - keys:T],
                            scale=1.0, scalar=-3.0e38, op0=ALU.add, op1=ALU.max,
                            accum_out=maxima[:, u % 2, t, c:c + 1])
                    last.then_inc(a_emptied, 1)
                if g % 2 == 1 and k == 2:
                    dve.wait_ge(a_emptied, 6 * (g + 1))
                    if u >= 2:
                        dve.wait_ge(side_filled, USE["maxima", u - 2] + 1)
                    hi, lo = neg_max[:, u % 2, :, :, 0], neg_max[:, u % 2, :, :, 1]
                    link(nc.vector.tensor_scalar(hi, maxima[:, u % 2, :, :], -1.0, None, ALU.mult))
                    nc.vector.scalar_tensor_tensor(out=lo, in0=maxima[:, u % 2, :, :], scalar=-1.0, in1=hi,
                                                   op0=ALU.mult, op1=ALU.subtract).then_inc(maxima_split, 1)

            dve.wait_ge(loaded_x, 16)
            begin_norm(0, x_sb[:, 0, :, :])
            dve.wait_ge(silu_exp, 1)
            link(nc.vector.tensor_scalar(c_exp[:, :], c_exp[:, :], 1.0, None, ALU.add))
            link(nc.vector.reciprocal(c_exp[:, :], c_exp[:, :]))
            nc.vector.tensor_tensor(c_silu[:, :], c_exp[:, :], c_sb[:, :], ALU.mult).then_inc(silu_done, 1)
            end_norm(0, x_sb[:, 0, :, :])
            dve.wait_ge(mod_copied, 1)
            for i in range(2):
                nc.vector.tensor_scalar(gate_sign[:, i, :], mod_sb[:, 3 * i + 2, :], 0.0, 2.0, ALU.is_ge, ALU.mult)
                link(nc.vector.tensor_scalar(gate_size[:, i, :], mod_sb[:, 3 * i + 2, :], -1.0, None, ALU.mult))
                link(nc.vector.tensor_tensor(gate_size[:, i, :], gate_size[:, i, :], mod_sb[:, 3 * i + 2, :], ALU.max))
                link(nc.vector.tensor_scalar(gate_size[:, i, :], gate_size[:, i, :], 0.25, None, ALU.max))
                link(nc.vector.scalar_tensor_tensor(out=gates[:, i, :], in0=gate_sign[:, i, :], scalar=-1.0,
                                                    in1=gate_size[:, i, :], op0=ALU.add, op1=ALU.mult))
                last = nc.vector.tensor_scalar(mod_sb[:, 3 * i + 1, :], mod_sb[:, 3 * i + 1, :], 1.0, None, ALU.add)
            last.then_inc(mod_ready, 1)
            dve.wait_ge(side_by_act, by_act("key", 0))
            link(nc.vector.tensor_tensor(rest[:, 1, :], proj[:, 1, :], parts[:, 1, 2, :], ALU.subtract))
            link(nc.vector.tensor_copy(parts[:, 1, 1, :], rest[:, 1, :]))
            nc.vector.tensor_tensor(parts[:, 1, 0, :], rest[:, 1, :], parts[:, 1, 1, :], ALU.subtract)\
                .then_inc(parts_done[1], 1)
            dve.wait_ge(loaded_causal, 16)
            norms = 1
            for g, k in PLACES:
                if 0 <= g < NP:
                    pass_a_max(g, k)
                for name, n in tasks(g, k):
                    task(name, n)
                    if name == "attn_back":
                        dve.wait_ge(side_by_dve, by_dve(name, n))
                        begin_norm(norms, x1[:, n % 2, :, :])
                        norms += 1
                if feed(g, k, 1) and feed(g, k, 1)[1] not in BY_POOL:
                    b, e = feed(g, k, 1)
                    count, value, at = masked_count(b, e)
                    dve.wait_ge(chosen_ready, 16 * (b + 1))
                    dve.wait_ge(side_by_act, by_act("norm2", b))
                    if fed_before(b, e):
                        dve.wait_ge(experts_fed, fed_before(b, e))
                    nc.vector.tensor_tensor(masked[:, at, :], h2T[:, :], chosen[:, e, :], ALU.mult)\
                        .then_inc(masked_by_dve, 1)
                if g >= 0 and g % 8 == 0 and k == 0 and g // 8 + 1 < B:
                    dve.wait_ge(loaded_w, LOADED_W)
                    begin_norm(norms, x_sb[:, g // 8 + 1, :, :])
                    norms += 1
                if g >= 0 and g % 8 == 1 and k == 1 and g // 8 + 1 < B:
                    end_norm(NORMS.index(("norm1", g // 8 + 1)), x_sb[:, g // 8 + 1, :, :])
                if g >= 8 and g % 8 == 7 and k == 2 and 0 <= g // 8 - 1 < B:
                    end_norm(NORMS.index(("norm2", g // 8 - 1)), x1[:, (g // 8 - 1) % 2, :, :])


def constants(B=4, T=512, H=16, E=8):
    import numpy as np

    def bf(v):
        return np.asarray(v).astype(np.dtype("bfloat16"))

    PAIRS = H // 2
    pos = bf(np.arange(T) - T // 2)
    block = np.arange(T) % 128 // 16
    qbias, kbias = bf(np.zeros((2, 6, PAIRS, T))), bf(np.zeros((2, 6, PAIRS, T)))
    for par in range(2):
        for pair in range(PAIRS):
            left = np.float32(2.0 ** (-8.0 * (2 * pair + par + 1) / H))
            for n in range(3):
                part = bf(left)
                left = np.float32(left - np.float32(part))
                qbias[par, 2 * n, pair] = part
                qbias[par, 2 * n + 1, pair] = pos
                kbias[par, 2 * n, pair] = pos
                kbias[par, 2 * n + 1, pair] = -part
    steps = np.arange(1, 8)[:, None]
    qmask = bf(np.tile(block[None, :] < steps, (1, PAIRS)))
    kmask = bf(np.tile(np.where(block[None, :] == steps, -16384.0, 0.0), (1, 2 * PAIRS)))
    causal = np.zeros((128, T), np.float32)
    causal[:, T - 128:] = np.where(np.arange(128)[None, :] > np.arange(128)[:, None], -1e30, 0.0)
    return {"qbias": qbias.reshape(2, 6, -1), "kbias": kbias.reshape(2, 6, -1), "kones": bf(np.ones((2, PAIRS * T))),
            "qmask": qmask, "kmask": kmask,
            "ident": np.eye(128, dtype=np.float32), "identb": bf(np.eye(128)), "causal": causal,
            "order": np.tile(np.arange(E, 0, -1, dtype=np.float32), (128, 1))}


def kernel(L0_attn_x, L0_attn_Wq, L0_attn_Wk, L0_attn_Wv, L0_attn_Wo, L0_ffn_gate_w, L0_ffn_expert_w, L0_c, L0_wmod):
    import numpy as np
    import concourse.bacc as bacc
    from concourse import mybir as mb
    from concourse.bass_utils import run_bass_kernel_spmd

    feature = np.array([(2 * pair + par) * 8 + d for par in range(2) for d in range(8) for pair in range(8)])
    arrays = {
        "x": L0_attn_x,
        "wqT": L0_attn_Wq[feature].T,
        "wkT": L0_attn_Wk[feature].T,
        "wvT": L0_attn_Wv.T,
        "woT": L0_attn_Wo.T,
        "gwT": L0_ffn_gate_w.T,
        "ewT": L0_ffn_expert_w.transpose(2, 0, 1),
        "cT": L0_c.T,
        "wmod": L0_wmod,
    }
    arrays = {k: np.ascontiguousarray(v) for k, v in {**arrays, **constants()}.items()}
    nc = bacc.Bacc("TRN2", target_bir_lowering=False, num_devices=1)
    args = [nc.dram_tensor(k, a.shape, mb.dt.from_np(a.dtype), kind="ExternalInput").ap() for k, a in arrays.items()]
    out = nc.dram_tensor("out", L0_attn_x.shape, mb.dt.float32, kind="ExternalOutput").ap()
    adaln_block(nc, *args, out)
    r = run_bass_kernel_spmd(nc, [arrays], core_ids=[0])
    return r.results[0]["out"]
```

```python
import concourse.bass as bass
from concourse import mybir
from contextlib import ExitStack


def adaln_block(nc, x, wqT, wkT, wvT, woT, gwT, ewT, cT, wmod, qbias, qmask, krows, place, ident, identb, causal,
                order, out):
    f32, bf16, i32 = mybir.dt.float32, mybir.dt.bfloat16, mybir.dt.int32
    ALU, ACT, AX = mybir.AluOpType, mybir.ActivationFunctionType, mybir.AxisListType

    B, T, D = x.shape
    H = 16
    DH = D // H
    E = gwT.shape[1]
    TT = T // 128
    PAIRS = H // 2
    QUADS = H // 4
    NP = B * PAIRS
    EPS = 1e-5
    R_HEAD = 48
    R_BIAS = 2 * R_HEAD
    R_MAX = R_BIAS + 12
    R_MASK = R_MAX + 4
    R_END = R_MASK + 7
    EARLY = 2
    QPART = [0, 1, 2, 0, 1, 0]
    KPART = [2, 1, 0, 1, 0, 0]
    NPROD = len(QPART)
    RUNS = [(0, 3), (3, 2), (5, 1)]
    FILL_START, FILL_NORM, FILL_AFTER, FILL_PLACE = 8, 2, {"norm1": 3, "key": 2}, 2
    LAG = 4
    AB, BB = 3, 2
    PW = 1280
    BSTEP = [[(t, t, 128, 128 * t) for t in range(TT)],
             [(0, 1, 384, 0), (2, 3, 128, 384)],
             [(1, 2, 256, 0)]]
    ASTEP = [[(3, 512, 0)], [(2, 384, 0), (0, 128, 384)], [(1, 256, 0)]]
    WIDTH = [512, 512, 256]
    P_AT = [0, 512, 1024]

    SIDE = {(7, 2): [("norm2", 1)], (0, 0): [("gate", 2)], (0, 2): [("gate_onehot", 2)],
            (2, 0): [("norm1", -1)], (2, 2): [("query", -1)], (3, 2): [("key", -1)], (4, 2): [("value", -1)],
            (5, 2): [("attn", 1)], (6, 1): [("outproj", 1)],
            (7, 0): [("expert_back", 2)]}
    FEED = {(3, 0): 0, (3, 1): 1, (4, 0): 2, (4, 1): 3, (5, 0): 4, (5, 1): 5, (6, 0): 6, (6, 2): 7}
    FEED_LAST = {(4, 1): 0, (4, 2): 1, (5, 1): 2, (6, 0): 3, (6, 2): 4, (7, 0): 5, (7, 1): 6, (7, 2): 7}
    BY_POOL = {(b, e) for b in range(B - 1) for e in ([4, 7] if b < B - 2 else [4, 5, 6, 7])}
    MASKS = [[(b, e) for b in range(B - 1) for e in range(E) if ((b, e) in BY_POOL) == pool] for pool in (False, True)]
    STORE, FETCH = {(3, 2): 0, (4, 2): 1}, {(4, 0): 0, (5, 0): 1}
    LAST = 8 * (B + 1) + 7 + 1
    VALUES = [[(0, 1, 256, 512)], [(0, 3, 128, 768), (2, 3, 128, 896)], [(1, 2, 256, 1024)],
              [(0, 0, 128, 0), (1, 1, 128, 128)], [(2, 2, 128, 256), (3, 3, 128, 384)]]

    LAST_VALUE = (len(VALUES) - 1, VALUES[-1][-1][0])

    def value_step(g, k):
        u, step = divmod(3 * (g - LAG - 1) + k - 2, 6)
        return (u, step) if 0 <= u < NP // 2 and step < len(VALUES) else None

    def feed(g, k, early=0):
        g, k = divmod(3 * g + k + early, 3)
        b = g // 8 - 2
        e = (FEED_LAST if b == B - 2 else FEED).get((g % 8, k))
        return (b, e) if e is not None and 0 <= b < B - 1 else None

    def tasks(g, k):
        found = []
        if g < 0:
            return [(name, 0) for name in ("norm1", "query", "key", "value")] if k == 0 else []
        if (g - LAG) % 2 == 1 and k == 1 and 0 <= (g - LAG - 3) // 2 < NP // 2:
            found.append(("heads_back", (g - LAG - 3) // 2))
        if g % 2 == 0 and k == 1 and 0 <= g // 2 - 1 < NP // 2:
            found.append(("maxima", g // 2 - 1))
        for name, ahead in SIDE.get((g % 8, k), []):
            b = g // 8 - ahead
            if b == B - 1 and name == "gate_onehot" or b >= B - 2 and name == "expert_back":
                continue
            if 0 <= b < B and not (ahead == -1 and b == 0):
                found.append((name, b))
        if (g, k) == (8 * B + 8, 1):
            found.append(("expert_back", B - 2))
        return found

    PLACES = [(-1, 0)] + [(g, k) for g in range(LAST) for k in range(3)]
    BY_DVE = {"heads_back", "outproj", "gate", "expert_back"}
    USES = [t for p in PLACES for t in tasks(*p)]
    USE = {t: n for n, t in enumerate(USES)}

    def emptied(n):
        dve = sum(name in BY_DVE for name, _ in USES[:n])
        return dve, n - dve

    def by_dve(name, n):
        return emptied(USE[name, n] + 1)[0]

    def by_act(name, n):
        return emptied(USE[name, n] + 1)[1]

    NORMS = [("norm1", 0)]
    for g in range(LAST):
        for k in range(3):
            if g % 8 == 0 and k == 1 and g // 8 + 1 < B:
                NORMS.append(("norm1", g // 8 + 1))
            NORMS += [("norm2", b) for name, b in tasks(g, k) if name == "outproj"]

    ctx = ExitStack()
    with ctx:
        def sb(name, shape, dt=f32):
            return ctx.enter_context(nc.sbuf_tensor(name, shape, dt))

        def pb(name):
            return ctx.enter_context(nc.psum_tensor(name, [128, 512], f32))

        def sem(name):
            return ctx.enter_context(nc.semaphore(name))

        wq_sb, wk_sb, wv_sb, wo_sb = (sb(n, [D, D]) for n in ("wq_sb", "wk_sb", "wv_sb", "wo_sb"))
        gw_sb = sb("gw_sb", [D, E])
        ew_in = sb("ew_in", [D, E, D])
        ew_sb = sb("ew_sb", [D, E, D])
        wmod_sb = sb("wmod_sb", [D, 6 * D])
        ident_sb = sb("ident_sb", [128, 128])
        identb_sb = sb("identb_sb", [128, 128], bf16)
        causal_sb = sb("causal_sb", [128, 512])
        idle_sb = sb("idle_sb", [128, 512], bf16)
        order_sb = sb("order_sb", [128, E])
        place_sb = sb("place_sb", [128, EARLY, 3, 3, R_BIAS], bf16)
        c_sb, c_exp, c_silu = sb("c_sb", [D, B]), sb("c_exp", [D, B]), sb("c_silu", [D, B])
        mod_sb = sb("mod_sb", [D, 6, B])
        gates = sb("gates", [D, 2, B])
        gate_sign, gate_size = sb("gate_sign", [D, 2, B]), sb("gate_size", [D, 2, B])
        x_sb = sb("x_sb", [128, B, TT, D])
        stats = sb("stats", [128, TT, 6])
        meanvar = sb("meanvar", [128, TT, 2])
        var_eps = sb("var_eps", [128, TT])
        half_bits = sb("half_bits", [128, TT], i32)
        rstd = sb("rstd", [128, TT])
        newton = sb("newton", [128, TT])
        normed = sb("normed", [128, TT, D])
        hT = sb("hT", [D, T])
        proj = sb("proj", [128, 2, T])
        rest = sb("rest", [128, 2, T])
        parts = sb("parts", [128, 2, 3, T], bf16)
        q_stack = [sb(f"q_stack{i}", [128, PAIRS * T], bf16) for i in range(2)]
        k_stack = [sb(f"k_stack{i}", [128, 2 * PAIRS * T], bf16) for i in range(2)]
        v_aug = sb("v_aug", [128, 2, TT, H, 32])
        scored = sb("scored", [128, 4, 512], bf16)
        maxima = sb("maxima", [128, 2, TT, 4])
        neg_max = sb("neg_max", [128, 2, TT, 4, 2], bf16)
        maxT = sb("maxT", [8, 2, T], bf16)
        probs = sb("probs", [128, 2, 4, PW])
        headsT = sb("headsT", [128, T])
        inv_sum = sb("inv_sum", [128, TT, 4])
        attn = sb("attn", [128, TT, D])
        attnT = sb("attnT", [D, T])
        backT = sb("backT", [D, T])
        wo_gated = sb("wo_gated", [D, B, D])
        ew_gated = sb("ew_gated", [D, E, D])
        x1 = sb("x1", [128, 2, TT, D])
        h2T = sb("h2T", [D, 2, T])
        choice = sb("choice", [128, TT, E])
        top = sb("top", [128, TT])
        is_top = sb("is_top", [128, TT, E])
        rank = sb("rank", [128, TT, E])
        onehot = sb("onehot", [128, TT, E], bf16)
        onehotT = sb("onehotT", [E, T], bf16)
        chosen = sb("chosen", [128, E, T], bf16)
        masked = sb("masked", [D, 4, T])
        result = sb("result", [128, TT, D])
        scratch = nc.dram_tensor("parts_scratch", [B, 2, 128, NPROD, T], bf16).ap()
        onehot_dram = nc.dram_tensor("onehot_scratch", [B, E, T], bf16).ap()

        a_bank = [pb(f"a_bank{i}") for i in range(AB)]
        b_bank = [pb(f"b_bank{i}") for i in range(BB)]
        v_bank = pb("v_bank")
        e_bank = pb("e_bank")
        side = pb("side")

        def key_bank(b):
            return side if b else a_bank[0]


        def bank_of_b(n):
            late = n - 6 * (NP - LAG)
            return b_bank[n % BB] if late < 0 else (b_bank + a_bank)[late % (AB + BB)]

        PLACE_BANKS = b_bank + [v_bank, e_bank]
        ALL_BANKS = a_bank + b_bank + [v_bank, e_bank, side]

        loaded_x = sem("loaded_x")
        loaded_c = sem("loaded_c")
        loaded_ident = sem("loaded_ident")
        loaded_place = sem("loaded_place")
        placed = sem("placed")
        idle_cleared = sem("idle_cleared")
        placed_by_act = sem("placed_by_act")
        loaded_mod = sem("loaded_mod")
        loaded_attn = sem("loaded_attn")
        loaded_causal = sem("loaded_causal")
        loaded_w = sem("loaded_w")
        loaded_rows = [sem(f"loaded_rows{i}") for i in range(2)]
        v_cleared = sem("v_cleared")
        k_cleared = [sem(f"k_cleared{i}") for i in range(2)]
        experts_ready = sem("experts_ready")
        silu_exp = sem("silu_exp")
        silu_done = sem("silu_done")
        mod_summed = sem("mod_summed")
        mod_copied = sem("mod_copied")
        mod_ready = sem("mod_ready")
        gates_ready = sem("gates_ready")
        gate_rows = sem("gate_rows")
        wo_ready = sem("wo_ready")
        ew_ready = sem("ew_ready")
        all_filled = sem("all_filled")
        selected = sem("selected")
        rsqrt_begun = sem("rsqrt_begun")
        rstd_ready = sem("rstd_ready")
        norm_done = sem("norm_done")
        side_filled = sem("side_filled")
        side_by_dve = sem("side_by_dve")
        side_by_act = sem("side_by_act")
        parts_done = [sem(f"parts_done{i}") for i in range(2)]
        parts_stored = [sem(f"parts_stored{i}") for i in range(2)]
        stacked = [sem(f"stacked{i}") for i in range(2)]
        a_filled = sem("a_filled")
        a_emptied = sem("a_emptied")
        b_filled = sem("b_filled")
        b_emptied = sem("b_emptied")
        maxima_split = sem("maxima_split")
        max_rows = [sem(f"max_rows{i}") for i in range(2)]
        zeroed = sem("zeroed")
        v_filled = sem("v_filled")
        v_emptied = sem("v_emptied")
        onehot_ready = sem("onehot_ready")
        onehot_stored = sem("onehot_stored")
        chosen_ready = sem("chosen_ready")
        masked_by_dve = sem("masked_by_dve")
        masked_by_pool = sem("masked_by_pool")
        experts_fed = sem("experts_fed")
        e_emptied = sem("e_emptied")
        stored = sem("stored")
        dve_step = sem("dve_step")
        pool_step = sem("pool_step")

        LOADED_ATTN, LOADED_W = 16 * 3, 16 * 6
        block = ctx.enter_context(nc.Block())

        def masked_count(b, e):
            pool = (b, e) in BY_POOL
            n = MASKS[pool].index((b, e))
            return (masked_by_pool if pool else masked_by_dve), n + 1, n % 2 + 2 * pool

        def fed_before(b, e):
            mine = MASKS[(b, e) in BY_POOL]
            n = mine.index((b, e)) - 2
            return 0 if n < 0 else E * mine[n][0] + mine[n][1] + 1

        @block.sync
        def _(sp):
            sp.dma_start(x_sb[:, 0, :, :], x[0].rearrange("(t p) d -> p t d", p=128)).then_inc(loaded_x, 16)
            sp.dma_start(c_sb[:, :], cT).then_inc(loaded_c, 16)
            sp.dma_start(ident_sb[:, :], ident).then_inc(loaded_ident, 16)
            sp.dma_start(wmod_sb[:, :], wmod).then_inc(loaded_mod, 16)
            for dst, src in ((wq_sb[:, :], wqT), (wk_sb[:, :], wkT), (wv_sb[:, :], wvT)):
                sp.dma_start(dst, src).then_inc(loaded_attn, 16)
            sp.dma_start(place_sb[:, :, :, :, :], place).then_inc(loaded_place, 16)

            def rows(i):
                sp.dma_start(q_stack[i][R_BIAS:R_MAX, :], qbias).then_inc(loaded_rows[i], 16)
                sp.dma_start(q_stack[i][R_MASK:R_END, :], qmask).then_inc(loaded_rows[i], 16)
                sp.dma_start(k_stack[i][R_BIAS:R_END, :], krows).then_inc(loaded_rows[i], 16)

            def store_parts(b, s):
                sp.wait_ge(parts_done[s], b + 1)
                for first, n in RUNS:
                    have = (2 - KPART[first]) if s else QPART[first]
                    sp.dma_start(scratch[b, s, :, first:first + n, :],
                                 parts[:, s, have:have + n, :]).then_inc(parts_stored[s], 16)

            def fetch_parts(b, s):
                st = (q_stack if s == 0 else k_stack)[b % 2]
                if b >= 2:
                    sp.wait_ge(b_filled, 3 * PAIRS * 2 * (b - 1))
                sp.wait_ge(parts_stored[s], 16 * len(RUNS) * (b + 1))
                if s == 1 and b < 2:
                    sp.wait_ge(k_cleared[b], 1)
                first = EARLY if b == 0 else 0
                for par in range(2):
                    at, base = R_HEAD * par, PAIRS * T * par * s
                    src = scratch[b, s, 64 * par + DH * first:64 * par + 64]
                    sp.dma_start(st[at:at + R_HEAD, base + first * T:base + PAIRS * T]
                                 .rearrange("r (j t) -> r j t", t=T), src.rearrange("(j d) n t -> (d n) j t", d=DH))\
                      .then_inc(stacked[b % 2], 16)

            sp.dma_start(causal_sb[:, :], causal).then_inc(loaded_causal, 16)
            rows(0)
            for dst, src in ((identb_sb[:, :], identb), (wo_sb[:, :], woT), (gw_sb[:, :], gwT), (order_sb[:, :], order),
                             (x_sb[:, 1:B, :, :], x[1:B].rearrange("b (t p) d -> p b t d", p=128)),
                             (ew_in[:, :, :], ewT)):
                sp.dma_start(dst, src).then_inc(loaded_w, 16)
            rows(1)
            store_parts(0, 0)
            store_parts(0, 1)
            fetch_parts(0, 0)
            fetch_parts(0, 1)

            for g, k in PLACES:
                if 0 <= g // 8 + 1 < B and g >= 0:
                    if (g % 8, k) in STORE:
                        store_parts(g // 8 + 1, STORE[g % 8, k])
                    if (g % 8, k) in FETCH:
                        fetch_parts(g // 8 + 1, FETCH[g % 8, k])
                if (g % 8, k) == (1, 0) and 0 <= g // 8 - 2 < B - 1:
                    n = g // 8 - 2
                    sp.wait_ge(onehot_stored, 16 * (n + 1))
                    if n >= 1:
                        sp.wait_ge(masked_by_dve, sum(b < n for b, e in MASKS[False]))
                        sp.wait_ge(masked_by_pool, sum(b < n for b, e in MASKS[True]))
                    sp.dma_start(chosen[:, :, :], onehot_dram[n].rearrange("e t -> (e t)").partition_broadcast(128))\
                      .then_inc(chosen_ready, 16)
                for name, n in tasks(g, k):
                    if name == "maxima":
                        sp.wait_ge(side_by_act, by_act(name, n))
                        for c in range(4):
                            pair = (4 * n + c) // 2 % PAIRS
                            at = R_MAX + 2 * (c % 2)
                            dst = q_stack[n // QUADS % 2][at:at + 2, pair * T:(pair + 1) * T]
                            sp.dma_start(dst, maxT[2 * c:2 * c + 2, n % 2, :]).then_inc(max_rows[n % 2], 16)
                    if name == "gate_onehot":
                        sp.wait_ge(side_by_act, by_act(name, n))
                        sp.dma_start(onehot_dram[n], onehotT[:, :]).then_inc(onehot_stored, 16)
                    if name == "expert_back":
                        sp.wait_ge(side_by_dve, by_dve(name, n))
                        sp.dma_start(out[n].rearrange("(t p) d -> p t d", p=128), result[:, :, :]).then_inc(stored, 16)
            for first in range(0, TT, 2):
                sp.wait_ge(selected, 4 * TT + 4 * first + 8)
                sp.dma_start(out[B - 1].rearrange("(t p) d -> p t d", p=128)[:, first:first + 2, :],
                             result[:, first:first + 2, :]).then_inc(stored, 16)
            sp.wait_ge(stored, 16 * (B + 1))

        @block.gpsimd
        def _(pool):
            steps = [0]

            def link(ins):
                steps[0] += 1
                ins.then_inc(pool_step, 1)
                pool.wait_ge(pool_step, steps[0])

            def newton_steps(n):
                pool.wait_ge(rsqrt_begun, n)
                for step in range(3):
                    link(nc.gpsimd.tensor_tensor(newton[:, :], rstd[:, :], rstd[:, :], ALU.mult))
                    link(nc.gpsimd.tensor_tensor(newton[:, :], newton[:, :], var_eps[:, :], ALU.mult))
                    link(nc.gpsimd.tensor_scalar(newton[:, :], newton[:, :], -0.5, 1.5, ALU.mult, ALU.add))
                    last = nc.gpsimd.tensor_tensor(rstd[:, :], rstd[:, :], newton[:, :], ALU.mult)
                    if step < 2:
                        link(last)
                last.then_inc(rstd_ready, 1)

            def split(s, b):
                pool.wait_ge(side_by_act, by_act("key" if s else "query", b))
                part = [parts[:, s, 2 - n if s else n, :] for n in range(3)]
                nc.gpsimd.tensor_tensor(part[1], proj[:, s, :], part[0], ALU.subtract)
                link(nc.gpsimd.tensor_tensor(rest[:, s, :], proj[:, s, :], part[0], ALU.subtract))
                nc.gpsimd.tensor_tensor(part[2], rest[:, s, :], part[1], ALU.subtract).then_inc(parts_done[s], 1)

            nc.gpsimd.memset(idle_sb[:, :].bitcast(f32), 0.0).then_inc(idle_cleared, 1)
            nc.gpsimd.memset(k_stack[0][0:R_BIAS, :].bitcast(f32), 0.0).then_inc(k_cleared[0], 1)
            norms = 1
            nc.gpsimd.memset(k_stack[1][0:R_BIAS, :].bitcast(f32), 0.0).then_inc(k_cleared[1], 1)
            nc.gpsimd.memset(v_aug[:, :, :, :, :], 0.0).then_inc(v_cleared, 1)
            pool.wait_ge(v_cleared, 1)
            nc.gpsimd.memset(v_aug[:, :, :, :, DH:DH + 1], 1.0).then_inc(v_cleared, 1)
            pool.wait_ge(loaded_w, LOADED_W)
            pool.wait_ge(loaded_ident, 16)
            nc.gpsimd.tensor_tensor(ew_sb[:, :, :], ew_in[:, :, :],
                                    ident_sb[:, :].unsqueeze(1).broadcast_to([128, E, 128]), ALU.add)\
                .then_inc(experts_ready, 1)
            for g in range(LAST):
                for k in range(3):
                    if k == 0 and 0 <= g - LAG < NP:
                        pair = g - LAG
                        for par in range(2):
                            pool.wait_ge(b_emptied, 6 * pair + par + 1)
                            diag = probs[:, pair // 2 % 2, 2 * (pair % 2) + par, 0:512]\
                                .rearrange("p (t q) -> p t q", t=TT)
                            nc.gpsimd.affine_select(out=diag, in_=diag, compare_op=ALU.is_ge, fill=0.0, base=0,
                                                    pattern=[[0, TT], [1, 128]], channel_multiplier=-1)\
                                .then_inc(zeroed, 1)
                    if g % 8 == 0 and k == 1 and g // 8 + 1 < B:
                        newton_steps(norms)
                        norms += 1
                    if feed(g, k, 1) and feed(g, k, 1) in BY_POOL:
                        b, e = feed(g, k, 1)
                        count, value, at = masked_count(b, e)
                        pool.wait_ge(chosen_ready, 16 * (b + 1))
                        pool.wait_ge(side_by_act, by_act("norm2", b))
                        if fed_before(b, e):
                            pool.wait_ge(experts_fed, fed_before(b, e))
                        nc.gpsimd.tensor_tensor(masked[:, at, :], h2T[:, b % 2, :], chosen[:, e, :], ALU.mult)\
                            .then_inc(masked_by_pool, 1)
                    for name, b in tasks(g, k):
                        if name == "query":
                            split(0, b)
                        if name == "key":
                            split(1, b)
                        if name == "outproj" and b < B - 1:
                            newton_steps(norms)
                            norms += 1

        @block.tensor
        def _(pe):
            def fill(task):
                dve, act = emptied(USE[task])
                if dve:
                    pe.wait_ge(side_by_dve, dve)
                if act:
                    pe.wait_ge(side_by_act, act)

            def turned(dst, src, idn, n=TT):
                for t in range(n):
                    last = nc.tensor.transpose(dst[:, 128 * t:128 * t + 128], src(t), idn)
                return last

            def feed_expert(e, b):
                count, value, at = masked_count(b, e)
                pe.wait_ge(count, value)
                if e == 0:
                    pe.wait_ge(experts_ready, 1)
                    if b >= 1:
                        pe.wait_ge(e_emptied, b)
                    else:
                        pe.wait_ge(ew_ready, 1)
                nc.tensor.matmul(e_bank[:, :], ew_sb[:, e, :], masked[:, at, :], start=(e == 0),
                                 stop=(e == E - 1)).then_inc(experts_fed, 1)

            def task(name, n):
                if (name, n) != ("key", 0):
                    fill((name, n))
                if (name, n) == ("gate", 0) or (name, n) == ("maxima", 0):
                    pe.wait_ge(loaded_w, LOADED_W)
                if name == "norm1" or name == "norm2":
                    pe.wait_ge(norm_done, NORMS.index((name, n)) + 1)
                    last = turned(side, lambda t: normed[:, t, :], ident_sb[:, :])
                if name in ("query", "key", "value"):
                    pe.wait_ge(side_by_act, by_act("norm1", n))
                if (name, n) == ("query", 0):
                    pe.wait_ge(loaded_attn, LOADED_ATTN)
                if (name, n) == ("value", 0):
                    pe.wait_ge(parts_done[0], 1)
                if name == "query":
                    last = nc.tensor.matmul(side[:, :], wq_sb[:, :], hT[:, :], start=True, stop=True)
                if name == "key":
                    last = nc.tensor.matmul(key_bank(n)[:, :], wk_sb[:, :], hT[:, :], start=True, stop=True)
                if name == "value":
                    for t in range(TT):
                        last = nc.tensor.matmul(side[:, 128 * t:128 * t + 128], hT[:, 128 * t:128 * t + 128],
                                                wv_sb[:, :], start=True, stop=True)
                if name == "maxima":
                    pe.wait_ge(maxima_split, n + 1)
                    last = turned(side[0:8, 0:256].bitcast(bf16),
                                  lambda t: neg_max[:, n % 2, t, :, :].rearrange("p c s -> p (c s)"), identb_sb[:, :])
                if name == "heads_back":
                    pe.wait_ge(v_emptied, n + 1)
                    last = turned(side, lambda t: headsT[:, 128 * t:128 * t + 128], ident_sb[:, :])
                if name == "attn":
                    pe.wait_ge(side_by_dve, by_dve("heads_back", QUADS * n + QUADS - 1))
                    last = turned(side, lambda t: attn[:, t, :], ident_sb[:, :])
                if name == "outproj":
                    pe.wait_ge(side_by_act, by_act("attn", n))
                    if n == 0:
                        pe.wait_ge(wo_ready, 1)
                    for t in range(TT):
                        last = nc.tensor.matmul(side[:, 128 * t:128 * t + 128], attnT[:, 128 * t:128 * t + 128],
                                                wo_gated[:, n, :], start=True, stop=True)
                if name == "gate":
                    pe.wait_ge(side_by_act, by_act("norm2", n))
                    for t in range(TT):
                        last = nc.tensor.matmul(side[:, E * t:E * t + E], h2T[:, n % 2, 128 * t:128 * t + 128],
                                                gw_sb[:, :], start=True, stop=True)
                if name == "gate_onehot":
                    pe.wait_ge(onehot_ready, n + 1)
                    last = turned(side[0:E, 0:256].bitcast(bf16), lambda t: onehot[:, t, :], identb_sb[:, :])
                if name == "expert_back":
                    pe.wait_ge(e_emptied, n + 1)
                    last = turned(side, lambda t: backT[:, 128 * t:128 * t + 128], ident_sb[:, :])
                last.then_inc(side_filled, 1)

            def keep_clock(n, bank):
                for _ in range(n):
                    nc.tensor.matmul(bank[:, :], idle_sb[:, 0:128], idle_sb[:, :], start=True, stop=True)

            def pass_a(g, k, par):
                if not 0 <= g < NP:
                    return
                b, pair = divmod(g, PAIRS)
                if g < EARLY and k == 0:
                    pe.wait_ge(placed_by_act, 3 * g + 2 + par)
                if g == EARLY or (g > EARLY and pair == 0):
                    if k == 0 and par == 0:
                        pe.wait_ge(stacked[b % 2], 16 * 4 * (b // 2 + 1))
                if pair == 0 and k == 0 and par == 0:
                    pe.wait_ge(loaded_rows[b % 2], 16 * 3)
                n = 6 * g + 2 * k + par
                if n >= AB:
                    pe.wait_ge(a_emptied, n - AB + 1)
                k_at = (PAIRS * par + pair) * T
                for t, keys, at in ASTEP[k]:
                    q0 = pair * T + 128 * t
                    last = nc.tensor.matmul(a_bank[n % AB][:, at:at + keys], q_stack[b % 2][0:R_MAX, q0:q0 + 128],
                                            k_stack[b % 2][0:R_MAX, k_at:k_at + keys], start=True, stop=True)
                last.then_inc(a_filled, 1)

            def pass_b(g, k, par):
                if not 0 <= g < NP:
                    return
                b, pair = divmod(g, PAIRS)
                if k == 0 and g % 2 == 0:
                    pe.wait_ge(max_rows[g // 2 % 2], 64 * (g // 4 + 1))
                n = 6 * g + 2 * k + par
                late = n - 6 * (NP - LAG)
                if BB <= late < AB + BB:
                    pe.wait_ge(a_emptied, 6 * NP)
                elif n >= BB:
                    pe.wait_ge(b_emptied, n - (BB if late < BB else AB + BB) + 1)
                rows = slice(0, R_END if k == 0 else R_MASK)
                for kt, qt, cols, at in BSTEP[k]:
                    q0, k0 = pair * T + 128 * qt, (PAIRS * par + pair) * T + 128 * kt
                    last = nc.tensor.matmul(bank_of_b(n)[:, at:at + cols], k_stack[b % 2][rows, k0:k0 + 128],
                                            q_stack[b % 2][rows, q0:q0 + cols], start=True, stop=True)
                last.then_inc(b_filled, 1)

            def values(u, step):
                b, quad = divmod(u, QUADS)
                if step == 0:
                    pe.wait_ge(b_emptied, 12 * u + 10)
                    pe.wait_ge(side_by_act, by_act("value", b))
                    if u >= 1:
                        pe.wait_ge(v_emptied, u)
                    else:
                        pe.wait_ge(wo_ready, 1)
                if step == 2:
                    pe.wait_ge(b_emptied, 12 * (u + 1))
                if step == 3:
                    pe.wait_ge(zeroed, 4 * (u + 1))
                for kt, qt, cols, at in VALUES[step]:
                    for c in range(4):
                        last = nc.tensor.matmul(v_bank[32 * c:32 * c + 32, 128 * qt:128 * qt + cols],
                                                v_aug[:, b % 2, kt, 4 * quad + c, :],
                                                probs[:, u % 2, c, at:at + cols],
                                                start=(step == 0), stop=((step, kt) == LAST_VALUE),
                                                tile_position=(0, 32 * c))
                if step == len(VALUES) - 1:
                    last.then_inc(v_filled, 1)

            pe.wait_ge(idle_cleared, 1)
            keep_clock(FILL_START, v_bank)
            pe.wait_ge(loaded_mod, 16)
            pe.wait_ge(silu_done, 1)
            for j in range(6):
                last = nc.tensor.matmul(e_bank[:, B * j:B * j + B], wmod_sb[:, D * j:D * j + D], c_silu[:, :],
                                        start=True, stop=True)
            last.then_inc(mod_summed, 1)
            keep_clock(FILL_NORM, v_bank)
            pe.wait_ge(loaded_ident, 16)
            for g, k in PLACES:
                here = tasks(g, k)
                if g == 0 and k < EARLY:
                    for which in range(3):
                        i, pair = 3 * k + which, k
                        if i == 0:
                            pe.wait_ge(loaded_place, 16)
                            pe.wait_ge(parts_done[0], 1)
                        if i == 1:
                            pe.wait_ge(parts_done[1], 1)
                        if i >= len(PLACE_BANKS):
                            pe.wait_ge(placed_by_act, i - len(PLACE_BANKS) + 1)
                        for n in range(3):
                            last = nc.tensor.matmul(PLACE_BANKS[i % len(PLACE_BANKS)][0:R_BIAS, :],
                                                    place_sb[:, pair, which, n, :], parts[:, min(which, 1), n, :],
                                                    start=(n == 0), stop=(n == 2))
                        last.then_inc(placed, 1)
                if (g, k) == (1, 0):
                    pe.wait_ge(placed_by_act, 3 * EARLY)
                    pe.wait_ge(gates_ready, 1)
                    for i, b, dst in [(0, b, v_bank[:, D * b:D * b + D]) for b in range(B)] + \
                            [(1, B - 1, e_bank[:, D:2 * D])]:
                        last = nc.tensor.matmul(dst, gates[:, i, b:b + 1].broadcast_to([D, 128]), ident_sb[:, :],
                                                start=True, stop=True)
                    last.then_inc(gate_rows, 1)
                pass_b(g - LAG, k, 0)
                pass_a(g, k, 0)
                if value_step(g, k):
                    values(*value_step(g, k))
                pass_b(g - LAG, k, 1)
                pass_a(g, k, 1)
                for name, n in here:
                    task(name, n)
                    if g < 0:
                        keep_clock(FILL_AFTER.get(name, 0), v_bank)
                if 1 <= g < LAG:
                    keep_clock(FILL_PLACE, b_bank[0])
                if feed(g, k):
                    b, e = feed(g, k)
                    feed_expert(e, b)
            pe.wait_ge(ew_ready, 1)
            for i in range(2 * TT):
                if i == 0:
                    pe.wait_ge(b_emptied, 6 * NP)
                if i == AB + BB:
                    pe.wait_ge(v_emptied, NP // 2)
                if i == AB + BB + 1:
                    pe.wait_ge(e_emptied, B - 1)
                if i == AB + BB + 2:
                    pe.wait_ge(side_by_dve, by_dve("expert_back", B - 2))
                half, t = divmod(i, TT)
                nc.tensor.matmul(ALL_BANKS[i][:, :], h2T[:, (B - 1) % 2, 128 * t:128 * t + 128],
                                 ew_gated[:, 4 * half:4 * half + 4, :].rearrange("p e d -> p (e d)"),
                                 start=True, stop=True).then_inc(all_filled, 1)

        @block.scalar
        def _(act):
            def task(name, n):
                if name in BY_DVE:
                    return
                act.wait_ge(side_filled, USE[name, n] + 1)
                if name == "norm1":
                    if n == 0:
                        act.wait_ge(mod_ready, 1)
                    ins = nc.scalar.activation(hT[:, :], side[:, :], ACT.Identity, bias=mod_sb[:, 0, n:n + 1],
                                               scale=mod_sb[:, 1, n:n + 1])
                if name in ("query", "key"):
                    s = int(name == "key")
                    if n >= 1:
                        act.wait_ge(parts_done[s], n)
                        act.wait_ge(parts_stored[s], 16 * len(RUNS) * n)
                    scale = 1.0 if s else float(DH) ** -0.5
                    bank = key_bank(n) if s else side
                    if n >= 1:
                        nc.scalar.activation(proj[:, s, :], bank[:, :], ACT.Copy, scale=scale)
                    ins = nc.scalar.activation(parts[:, s, 2 if s else 0, :], bank[:, :], ACT.Copy, scale=scale)
                if name == "value":
                    act.wait_ge(v_cleared, 2)
                    if n >= 2:
                        act.wait_ge(v_filled, QUADS * (n - 1))
                    ins = nc.scalar.activation(v_aug[:, n % 2, :, :, 0:DH],
                                               side[:, :].rearrange("p (t h d) -> p t h d", t=TT, h=H), ACT.Copy)
                if name == "maxima":
                    if n >= 2:
                        act.wait_ge(max_rows[n % 2], 64 * (n // 2))
                    ins = nc.scalar.activation(maxT[:, n % 2, :], side[0:8, 0:256].bitcast(bf16), ACT.Copy)
                if name == "attn":
                    ins = nc.scalar.activation(attnT[:, :], side[:, :], ACT.Copy)
                if name == "norm2":
                    if n >= 2:
                        act.wait_ge(experts_fed, E * (n - 1))
                    ins = nc.scalar.activation(h2T[:, n % 2, :], side[:, :], ACT.Identity, bias=mod_sb[:, 3, n:n + 1],
                                               scale=mod_sb[:, 4, n:n + 1])
                if name == "gate_onehot":
                    if n >= 1:
                        act.wait_ge(onehot_stored, 16 * n)
                    ins = nc.scalar.activation(onehotT[:, :], side[0:E, 0:256].bitcast(bf16), ACT.Copy)
                ins.then_inc(side_by_act, 1)

            def exps(g, k):
                u = g // 2
                for par in range(2):
                    n = 6 * g + 2 * k + par
                    act.wait_ge(b_filled, n + 1)
                    if u >= 2 and g % 2 == 0 and k == 0 and par == 0:
                        act.wait_ge(v_filled, u - 1)
                    nc.scalar.activation(probs[:, u % 2, 2 * (g % 2) + par, P_AT[k]:P_AT[k] + WIDTH[k]],
                                         bank_of_b(n)[:, 0:WIDTH[k]], ACT.Exp).then_inc(b_emptied, 1)

            act.wait_ge(loaded_c, 16)
            nc.scalar.activation(c_exp[:, :], c_sb[:, :], ACT.Exp, scale=-1.0).then_inc(silu_exp, 1)
            act.wait_ge(mod_summed, 1)
            nc.scalar.activation(mod_sb[:, :, :], e_bank[:, 0:6 * B].rearrange("p (j b) -> p j b", j=6), ACT.Copy)\
                .then_inc(mod_copied, 1)
            for g, k in PLACES:
                if g == 0 and k < EARLY:
                    for which in range(3):
                        i, pair = 3 * k + which, k
                        if i == 1:
                            act.wait_ge(k_cleared[0], 1)
                        act.wait_ge(placed, i + 1)
                        stack = k_stack[0] if which else q_stack[0]
                        at = (max(which - 1, 0) * PAIRS + pair) * T
                        nc.scalar.activation(stack[0:R_BIAS, at:at + T], PLACE_BANKS[i % len(PLACE_BANKS)][0:R_BIAS, :],
                                             ACT.Copy).then_inc(placed_by_act, 1)
                if 0 <= g - LAG < NP:
                    exps(g - LAG, k)
                if value_step(g, k) and value_step(g, k)[1] == len(VALUES) - 1:
                    u = value_step(g, k)[0]
                    act.wait_ge(v_filled, u + 1)
                    if u >= 1:
                        act.wait_ge(side_by_dve, by_dve("heads_back", u - 1))
                    nc.scalar.activation(headsT[:, :], v_bank[:, :], ACT.Copy).then_inc(v_emptied, 1)
                for name, n in tasks(g, k):
                    task(name, n)
                if feed(g, k) and feed(g, k)[1] == E - 1:
                    b = feed(g, k)[0]
                    act.wait_ge(experts_fed, E * (b + 1))
                    nc.scalar.activation(backT[:, :], e_bank[:, :], ACT.Copy, scale=gates[:, 1, b:b + 1])\
                        .then_inc(e_emptied, 1)

        @block.vector
        def _(dve):
            steps = [0]

            def link(ins):
                steps[0] += 1
                ins.then_inc(dve_step, 1)
                dve.wait_ge(dve_step, steps[0])

            def silu():
                dve.wait_ge(silu_exp, 1)
                link(nc.vector.tensor_scalar(c_exp[:, :], c_exp[:, :], 1.0, None, ALU.add))
                link(nc.vector.reciprocal(c_exp[:, :], c_exp[:, :]))
                nc.vector.tensor_tensor(c_silu[:, :], c_exp[:, :], c_sb[:, :], ALU.mult).then_inc(silu_done, 1)

            def begin_norm(n, src):
                if n >= 1:
                    dve.wait_ge(norm_done, n)
                for t in range(TT):
                    last = nc.vector.bn_stats(stats[:, t, :], src[:, t, :])
                link(last)
                if n == 0:
                    silu()
                for t in range(TT):
                    last = nc.vector.bn_aggr(meanvar[:, t, :], stats[:, t, :])
                link(last)
                link(nc.vector.tensor_scalar(var_eps[:, :], meanvar[:, :, 1], EPS, None, ALU.add))
                link(nc.vector.tensor_scalar(half_bits[:, :], var_eps[:, :].bitcast(i32), 1, None,
                                             ALU.logical_shift_right))
                last = nc.vector.tensor_scalar(rstd[:, :].bitcast(i32), half_bits[:, :], -1.0, float(0x5F3759DF),
                                               ALU.mult, ALU.add)
                if 0 < n < len(NORMS) - 1:
                    last.then_inc(rsqrt_begun, 1)
                    return
                link(last)
                for step in range(3):
                    link(nc.vector.scalar_tensor_tensor(out=newton[:, :], in0=rstd[:, :], scalar=-0.5, in1=rstd[:, :],
                                                        op0=ALU.mult, op1=ALU.mult))
                    link(nc.vector.tensor_tensor(newton[:, :], newton[:, :], var_eps[:, :], ALU.mult))
                    link(nc.vector.scalar_tensor_tensor(out=rstd[:, :], in0=newton[:, :], scalar=1.5, in1=rstd[:, :],
                                                        op0=ALU.add, op1=ALU.mult))

            def end_norm(n, src):
                if 0 < n < len(NORMS) - 1:
                    dve.wait_ge(rstd_ready, n)
                if n >= 1:
                    dve.wait_ge(side_filled, USE[NORMS[n - 1]] + 1)
                for t in range(TT):
                    last = nc.vector.tensor_scalar(normed[:, t, :], src[:, t, :], meanvar[:, t, 0:1],
                                                   rstd[:, t:t + 1], ALU.subtract, ALU.mult)
                last.then_inc(norm_done, 1)

            def task(name, n):
                if name not in BY_DVE:
                    return
                dve.wait_ge(side_filled, USE[name, n] + 1)
                if name == "heads_back":
                    b, quad = divmod(n, QUADS)
                    if quad == 0 and b >= 1:
                        dve.wait_ge(side_by_act, by_act("attn", b - 1))
                    got = side[:, :].rearrange("p (t c w) -> p t c w", t=TT, c=4)
                    link(nc.vector.reciprocal(inv_sum[:, :, :], got[:, :, :, DH]))
                    dst = attn[:, :, 32 * quad:32 * quad + 32].rearrange("p t (c d) -> p t c d", c=4)
                    nc.vector.tensor_tensor(dst, got[:, :, :, 0:DH],
                                            inv_sum[:, :, :].unsqueeze(3).broadcast_to([128, TT, 4, DH]),
                                            ALU.mult).then_inc(side_by_dve, 1)
                if name == "outproj":
                    nc.vector.tensor_tensor(x1[:, n % 2, :, :], side[:, :].rearrange("p (t d) -> p t d", t=TT),
                                            x_sb[:, n, :, :], ALU.add).then_inc(side_by_dve, 1)
                if name == "gate":
                    got = side[:, 0:TT * E].rearrange("p (t e) -> p t e", t=TT)
                    link(nc.vector.reduce_max(top[:, :], got, AX.X))
                    nc.vector.tensor_tensor(is_top[:, :, :], got, top[:, :].unsqueeze(2).broadcast_to([128, TT, E]),
                                            ALU.is_equal).then_inc(side_by_dve, 1)
                    dve.wait_ge(side_by_dve, by_dve(name, n))
                    link(nc.vector.tensor_tensor(rank[:, :, :], is_top[:, :, :],
                                                 order_sb[:, :].unsqueeze(1).broadcast_to([128, TT, E]), ALU.mult))
                    link(nc.vector.reduce_max(top[:, :], rank[:, :, :], AX.X))
                    nc.vector.tensor_tensor((choice if n == B - 1 else onehot)[:, :, :], rank[:, :, :],
                                            top[:, :].unsqueeze(2).broadcast_to([128, TT, E]), ALU.is_equal)\
                        .then_inc(onehot_ready, 1)
                if name == "expert_back":
                    if n >= 1:
                        dve.wait_ge(stored, 16 * n)
                    nc.vector.tensor_tensor(result[:, :, :], side[:, :].rearrange("p (t d) -> p t d", t=TT),
                                            x1[:, n % 2, :, :], ALU.add).then_inc(side_by_dve, 1)

            def pass_a_max(g, k):
                u = g // 2
                for par in range(2):
                    n = 6 * g + 2 * k + par
                    c = 2 * (g % 2) + par
                    if n >= 4:
                        dve.wait_ge(a_emptied, n - 3)
                    dve.wait_ge(a_filled, n + 1)
                    for t, keys, at in ASTEP[k]:
                        last = nc.vector.tensor_tensor_reduce(
                            out=scored[:, n % 4, at:at + keys], in0=a_bank[n % AB][:, at:at + keys], in1=causal_sb[:, T - keys:T],
                            scale=1.0, scalar=-3.0e38, op0=ALU.add, op1=ALU.max,
                            accum_out=maxima[:, u % 2, t, c:c + 1])
                    last.then_inc(a_emptied, 1)
                if g % 2 == 1 and k == 2:
                    dve.wait_ge(a_emptied, 6 * (g + 1))
                    if u >= 2:
                        dve.wait_ge(side_filled, USE["maxima", u - 2] + 1)
                    hi, lo = neg_max[:, u % 2, :, :, 0], neg_max[:, u % 2, :, :, 1]
                    link(nc.vector.tensor_scalar(hi, maxima[:, u % 2, :, :], -1.0, None, ALU.mult))
                    nc.vector.scalar_tensor_tensor(out=lo, in0=maxima[:, u % 2, :, :], scalar=-1.0, in1=hi,
                                                   op0=ALU.mult, op1=ALU.subtract).then_inc(maxima_split, 1)

            dve.wait_ge(loaded_x, 16)
            begin_norm(0, x_sb[:, 0, :, :])
            end_norm(0, x_sb[:, 0, :, :])
            dve.wait_ge(mod_copied, 1)
            for i in range(2):
                last = nc.vector.tensor_scalar(mod_sb[:, 3 * i + 1, :], mod_sb[:, 3 * i + 1, :], 1.0, None, ALU.add)
            last.then_inc(mod_ready, 1)
            for i in range(2):
                nc.vector.tensor_scalar(gate_sign[:, i, :], mod_sb[:, 3 * i + 2, :], 0.0, 2.0, ALU.is_ge, ALU.mult)
                link(nc.vector.tensor_scalar(gate_size[:, i, :], mod_sb[:, 3 * i + 2, :], -1.0, None, ALU.mult))
                link(nc.vector.tensor_tensor(gate_size[:, i, :], gate_size[:, i, :], mod_sb[:, 3 * i + 2, :], ALU.max))
                link(nc.vector.tensor_scalar(gate_size[:, i, :], gate_size[:, i, :], 0.25, None, ALU.max))
                last = nc.vector.scalar_tensor_tensor(out=gates[:, i, :], in0=gate_sign[:, i, :], scalar=-1.0,
                                                      in1=gate_size[:, i, :], op0=ALU.add, op1=ALU.mult)
            last.then_inc(gates_ready, 1)
            for s, name in ((0, "query"), (1, "key")):
                dve.wait_ge(side_by_act, by_act(name, 0))
                part = [parts[:, s, 2 - n if s else n, :] for n in range(3)]
                bank, scale = (key_bank(0), 1.0) if s else (side, float(DH) ** -0.5)
                rested = nc.vector.scalar_tensor_tensor(out=rest[:, s, :], in0=bank[:, :], scalar=scale, in1=part[0],
                                                        op0=ALU.mult, op1=ALU.subtract)
                link(rested)
                link(nc.vector.tensor_copy(part[1], rest[:, s, :]))
                nc.vector.tensor_tensor(part[2], rest[:, s, :], part[1], ALU.subtract).then_inc(parts_done[s], 1)
            dve.wait_ge(loaded_causal, 16)
            norms = 1
            for g, k in PLACES:
                if 0 <= g < NP:
                    pass_a_max(g, k)
                for name, n in tasks(g, k):
                    task(name, n)
                    if name == "outproj":
                        dve.wait_ge(side_by_dve, by_dve(name, n))
                        begin_norm(norms, x1[:, n % 2, :, :])
                        norms += 1
                if feed(g, k, 1) and feed(g, k, 1) not in BY_POOL:
                    b, e = feed(g, k, 1)
                    count, value, at = masked_count(b, e)
                    dve.wait_ge(chosen_ready, 16 * (b + 1))
                    dve.wait_ge(side_by_act, by_act("norm2", b))
                    if fed_before(b, e):
                        dve.wait_ge(experts_fed, fed_before(b, e))
                    nc.vector.tensor_tensor(masked[:, at, :], h2T[:, b % 2, :], chosen[:, e, :], ALU.mult)\
                        .then_inc(masked_by_dve, 1)
                if (g, k) == (2, 0):
                    dve.wait_ge(gate_rows, 1)
                    nc.vector.tensor_tensor(wo_gated[:, :, :], v_bank[:, :].rearrange("p (b d) -> p b d", b=B),
                                            wo_sb[:, :].unsqueeze(1).broadcast_to([D, B, D]), ALU.mult)\
                        .then_inc(wo_ready, 1)
                    dve.wait_ge(experts_ready, 1)
                    nc.vector.tensor_tensor(ew_gated[:, :, :], ew_sb[:, :, :],
                                            e_bank[:, D:2 * D].unsqueeze(1).broadcast_to([D, E, D]), ALU.mult)\
                        .then_inc(ew_ready, 1)
                if g >= 0 and g % 8 == 0 and k == 0 and g // 8 + 1 < B:
                    dve.wait_ge(loaded_w, LOADED_W)
                    begin_norm(norms, x_sb[:, g // 8 + 1, :, :])
                    norms += 1
                if g >= 0 and g % 8 == 1 and k == 1 and g // 8 + 1 < B:
                    end_norm(NORMS.index(("norm1", g // 8 + 1)), x_sb[:, g // 8 + 1, :, :])
                if g >= 8 and g % 8 == 7 and k == 1 and 0 <= g // 8 - 1 < B:
                    end_norm(NORMS.index(("norm2", g // 8 - 1)), x1[:, (g // 8 - 1) % 2, :, :])

            dve.wait_ge(onehot_ready, B)
            dve.wait_ge(stored, 16 * (B - 1))
            done = 0
            for half in range(2):
                for first in range(0, TT, 2):
                    dve.wait_ge(all_filled, TT * half + first + 2)
                    for e in range(4):
                        for t in (first, first + 1):
                            if done > 1:
                                dve.wait_ge(selected, done - 1)
                            before = x1[:, (B - 1) % 2, t, :] if half == 0 and e == 0 else result[:, t, :]
                            nc.vector.scalar_tensor_tensor(
                                out=result[:, t, :], in0=ALL_BANKS[TT * half + t][:, D * e:D * e + D],
                                scalar=choice[:, t, 4 * half + e:4 * half + e + 1], in1=before,
                                op0=ALU.mult, op1=ALU.add).then_inc(selected, 1)
                            done += 1


def constants(B=4, T=512, H=16, E=8):
    import numpy as np

    def bf(v):
        return np.asarray(v).astype(np.dtype("bfloat16"))

    PAIRS = H // 2
    pos = bf(np.arange(T) - T // 2)
    block = np.arange(T) % 128 // 16
    qbias, kbias = bf(np.zeros((2, 6, PAIRS, T))), bf(np.zeros((2, 6, PAIRS, T)))
    for par in range(2):
        for pair in range(PAIRS):
            left = np.float32(2.0 ** (-8.0 * (2 * pair + par + 1) / H))
            for n in range(3):
                part = bf(left)
                left = np.float32(left - np.float32(part))
                qbias[par, 2 * n, pair] = part
                qbias[par, 2 * n + 1, pair] = pos
                kbias[par, 2 * n, pair] = pos
                kbias[par, 2 * n + 1, pair] = -part
    steps = np.arange(1, 8)[:, None]
    qmask = bf(np.tile(block[None, :] < steps, (1, PAIRS)))
    kmask = bf(np.tile(np.where(block[None, :] == steps, -16384.0, 0.0), (1, 2 * PAIRS)))
    causal = np.zeros((128, T), np.float32)
    causal[:, T - 128:] = np.where(np.arange(128)[None, :] > np.arange(128)[:, None], -1e30, 0.0)
    half = PAIRS * T
    krows = bf(np.zeros((23, 2 * half)))
    for par in range(2):
        krows[6 * par:6 * par + 6, half * par:half * par + half] = kbias[par].reshape(6, -1)
        krows[12 + 2 * par:14 + 2 * par, half * par:half * par + half] = bf(1.0)
    krows[16:] = kmask
    place = np.zeros((128, 2, 3, 3, 96), np.float32)
    for pair in range(2):
        for par in range(2):
            for d in range(8):
                for n, (qpart, kpart) in enumerate(zip([0, 1, 2, 0, 1, 0], [2, 1, 0, 1, 0, 0])):
                    feature, row = 64 * par + 8 * pair + d, 48 * par + 6 * d + n
                    place[feature, pair, 0, qpart, row] = 1.0
                    place[feature, pair, 1 + par, 2 - kpart, row] = 1.0
    return {"qbias": qbias.reshape(12, -1), "qmask": qmask, "krows": krows, "place": bf(place),
            "ident": np.eye(128, dtype=np.float32), "identb": bf(np.eye(128)), "causal": causal,
            "order": np.tile(np.arange(E, 0, -1, dtype=np.float32), (128, 1))}


def kernel(L0_attn_x, L0_attn_Wq, L0_attn_Wk, L0_attn_Wv, L0_attn_Wo, L0_ffn_gate_w, L0_ffn_expert_w, L0_c, L0_wmod):
    import numpy as np
    import concourse.bacc as bacc
    from concourse import mybir as mb
    from concourse.bass_utils import run_bass_kernel_spmd

    feature = np.array([(2 * pair + par) * 8 + d for par in range(2) for pair in range(8) for d in range(8)])
    arrays = {
        "x": L0_attn_x,
        "wqT": L0_attn_Wq[feature].T,
        "wkT": L0_attn_Wk[feature].T,
        "wvT": L0_attn_Wv.T,
        "woT": L0_attn_Wo.T,
        "gwT": L0_ffn_gate_w.T,
        "ewT": L0_ffn_expert_w.transpose(2, 0, 1),
        "cT": L0_c.T,
        "wmod": L0_wmod,
    }
    arrays = {k: np.ascontiguousarray(v) for k, v in {**arrays, **constants()}.items()}
    nc = bacc.Bacc("TRN2", target_bir_lowering=False, num_devices=1)
    args = [nc.dram_tensor(k, a.shape, mb.dt.from_np(a.dtype), kind="ExternalInput").ap() for k, a in arrays.items()]
    out = nc.dram_tensor("out", L0_attn_x.shape, mb.dt.float32, kind="ExternalOutput").ap()
    adaln_block(nc, *args, out)
    r = run_bass_kernel_spmd(nc, [arrays], core_ids=[0])
    return r.results[0]["out"]
```
